# Optimizing a Trainium2 kernel written in Bass

```python
import numpy as np
import jax
import jax.numpy as jnp

def _softmax(x, axis=-1):
    return jax.nn.softmax(x, axis=axis)

def _gelu(x):
    return jax.nn.gelu(x, approximate=True)

def _silu(x):
    return jax.nn.silu(x)

def _sigmoid(x):
    return jax.nn.sigmoid(x)

def _layernorm(x, axis=-1, eps=1e-05):
    m = jnp.mean(x, axis=axis, keepdims=True)
    v = jnp.var(x, axis=axis, keepdims=True)
    return (x - m) / jnp.sqrt(v + eps)

def _scatter_add(tgt, idx, src, axis=0):
    return tgt.at[idx].add(src)

def _segment_sum(src, seg, n):
    return jax.ops.segment_sum(src, seg, n)
kernel_name = 'mk_xattn_ffn_d1_seqx_r4_a5bc08'

def setup_inputs(seed: int=0):
    np.random.seed(seed)
    _w = jnp.asarray

    def _rec_inputs():
        import jax
        import jax.numpy as jnp
        _rk = jax.random.key(seed)
        x = -0.000917 + 0.9994 * jax.random.normal(jax.random.fold_in(_rk, 1), (8, 256, 256), jnp.float32)
        _lenS = 256 - jax.random.randint(jax.random.fold_in(_rk, 7), (8,), 0, max(1, 256 // 4) + 1, jnp.int32)
        _lenS2 = 77 - jax.random.randint(jax.random.fold_in(_rk, 8), (8,), 0, max(1, 77 // 4) + 1, jnp.int32)
        _ctx_1024P = jax.random.normal(jax.random.fold_in(_rk, 11), (8, 16, 256), jnp.float32)
        _ctx_1024c = jax.random.dirichlet(jax.random.fold_in(_rk, 511), 0.3 * jnp.ones((16,), jnp.float32), (8, 77))
        _ctx_1024t = jnp.einsum('bsk,bkd->bsd', _ctx_1024c, _ctx_1024P)
        _ctx_1024t = _ctx_1024t * jax.lax.rsqrt(jnp.mean(jnp.square(_ctx_1024t)) + 1e-12) * 0.953939
        ctx_1024 = 0.000579855 + 1.00008 * (_ctx_1024t + 0.3 * jax.random.normal(jax.random.fold_in(_rk, 611), (8, 77, 256), jnp.float32))
        _validS = jnp.arange(256)[None, :] < _lenS[:, None]
        _validS2 = jnp.arange(77)[None, :] < _lenS2[:, None]
        _causal = jnp.tril(jnp.ones((256, 256), dtype=bool))
        mask_Bx1xSxS2_ik1 = jnp.where(jnp.broadcast_to(_validS2[:, None, None, :], (8, 1, 256, 77)), 1, 0).astype(jnp.int32)
        return (x, ctx_1024, mask_Bx1xSxS2_ik1)
    x, ctx_1024, mask_Bx1xSxS2_ik1 = _rec_inputs()

    def _L0_xattn_setup():
        import jax, jax.numpy as jnp
        import numpy as np
        B, S, D, H = (2, 512, 256, 16)
        HD = D // H
        SCALE = HD ** (-0.5)
        key = jax.random.key(seed)
        ks = jax.random.split(key, 12)

        def lin(kw, kb):
            w = jax.random.normal(kw, (D, D), jnp.float32) * D ** (-0.5)
            b = jax.random.normal(kb, (D,), jnp.float32) * 0.01
            return (w, b)
        Wq, bq = lin(ks[0], ks[1])
        Wk, bk = lin(ks[2], ks[3])
        Wv, bv = lin(ks[4], ks[5])
        Wo, bo = lin(ks[6], ks[7])
        q = jax.random.normal(ks[8], (B, S, D), jnp.float32)
        k = jax.random.normal(ks[9], (B, S, D), jnp.float32)
        v = jax.random.normal(ks[10], (B, S, D), jnp.float32)
        mask = jax.random.randint(ks[11], (B, 1, S, S), 0, 2, jnp.int32)
        return {'q': q, 'k': k, 'v': v, 'mask': mask, 'Wq': Wq, 'bq': bq, 'Wk': Wk, 'bk': bk, 'Wv': Wv, 'bv': bv, 'Wo': Wo, 'bo': bo}
    _L0_xattn_all = _L0_xattn_setup()
    _L0_xattn_in = {k: v for k, v in _L0_xattn_all.items() if k in ('Wq', 'bq', 'Wk', 'bk', 'Wv', 'bv', 'Wo', 'bo')}
    del _L0_xattn_all

    def _L0_ffn_setup():
        import jax, jax.numpy as jnp
        import numpy as np
        E = 16
        H = 256
        F = 512
        TOP_K = 1
        B, S = (2, 256)
        key = jax.random.key(seed)
        ks = jax.random.split(key, 7)
        s = 0.02
        return {'hidden_states': jax.random.normal(ks[0], (B, S, H), jnp.float32), 'w_router': jax.random.normal(ks[1], (E, H), jnp.float32) * s, 'gate_up_proj': jax.random.normal(ks[2], (E, H, 2 * F), jnp.float32) * s, 'down_proj': jax.random.normal(ks[3], (E, F, H), jnp.float32) * s, 'w_gate': jax.random.normal(ks[4], (F, H), jnp.float32) * s, 'w_up': jax.random.normal(ks[5], (F, H), jnp.float32) * s, 'w_down': jax.random.normal(ks[6], (H, F), jnp.float32) * s}
    _L0_ffn_all = _L0_ffn_setup()
    _L0_ffn_in = {k: v for k, v in _L0_ffn_all.items() if k in ('w_router', 'gate_up_proj', 'down_proj', 'w_gate', 'w_up', 'w_down')}
    del _L0_ffn_all
    return {'x': x, 'ctx_1024': ctx_1024, 'mask_Bx1xSxS2_ik1': mask_Bx1xSxS2_ik1, 'L0_xattn_Wq': _L0_xattn_in['Wq'], 'L0_xattn_bq': _L0_xattn_in['bq'], 'L0_xattn_Wk': _L0_xattn_in['Wk'], 'L0_xattn_bk': _L0_xattn_in['bk'], 'L0_xattn_Wv': _L0_xattn_in['Wv'], 'L0_xattn_bv': _L0_xattn_in['bv'], 'L0_xattn_Wo': _L0_xattn_in['Wo'], 'L0_xattn_bo': _L0_xattn_in['bo'], 'L0_ffn_w_router': _L0_ffn_in['w_router'], 'L0_ffn_gate_up_proj': _L0_ffn_in['gate_up_proj'], 'L0_ffn_down_proj': _L0_ffn_in['down_proj'], 'L0_ffn_w_gate': _L0_ffn_in['w_gate'], 'L0_ffn_w_up': _L0_ffn_in['w_up'], 'L0_ffn_w_down': _L0_ffn_in['w_down']}

def reference(x, ctx_1024, mask_Bx1xSxS2_ik1, L0_xattn_Wq, L0_xattn_bq, L0_xattn_Wk, L0_xattn_bk, L0_xattn_Wv, L0_xattn_bv, L0_xattn_Wo, L0_xattn_bo, L0_ffn_w_router, L0_ffn_gate_up_proj, L0_ffn_down_proj, L0_ffn_w_gate, L0_ffn_w_up, L0_ffn_w_down):
    import jax
    import jax.numpy as jnp

    def _L0_xattn_ref(q, k, v, mask, Wq, bq, Wk, bk, Wv, bv, Wo, bo):
        import jax, jax.numpy as jnp
        import numpy as np
        B, S, D, H = (2, 512, 256, 16)
        HD = D // H
        SCALE = HD ** (-0.5)
        b = q.shape[0]

        def proj(x, W, bias):
            y = x @ W.T + bias
            return y.reshape(b, -1, H, HD).transpose(0, 2, 1, 3)
        qh, kh, vh = (proj(q, Wq, bq), proj(k, Wk, bk), proj(v, Wv, bv))
        scores = jnp.einsum('bhqd,bhkd->bhqk', qh, kh) * SCALE
        scores = jnp.where(mask == 0, jnp.float32(-1000000000.0), scores)
        attn = jax.nn.softmax(scores, axis=-1)
        out = jnp.einsum('bhqk,bhkd->bhqd', attn, vh)
        out = out.transpose(0, 2, 1, 3).reshape(b, -1, H * HD)
        return out @ Wo.T + bo

    def _L0_ffn_ref(hidden_states, w_router, gate_up_proj, down_proj, w_gate, w_up, w_down):
        import jax, jax.numpy as jnp
        import numpy as np
        E = 16
        H = 256
        F = 512
        TOP_K = 1
        B, S = (2, 256)
        b, s, h = hidden_states.shape
        x = hidden_states.reshape(-1, h)
        logits = x @ w_router.T
        _, top_idx = jax.lax.top_k(logits, TOP_K)
        mask = jax.nn.one_hot(top_idx, E, dtype=logits.dtype).sum(axis=1)
        scores = jax.nn.sigmoid(logits) * mask
        masked_inputs = scores.T[:, :, None] * x[None, :, :]
        gate_up = jnp.einsum('eth,ehf->etf', masked_inputs, gate_up_proj)
        gate, up = jnp.split(gate_up, 2, axis=-1)
        expert_out = jnp.einsum('etf,efh->eth', up * jax.nn.silu(gate), down_proj)
        shared = jax.nn.silu(x @ w_gate.T) * (x @ w_up.T) @ w_down.T
        out = shared + expert_out.sum(axis=0)
        return out.reshape(b, s, h)
    x = x + _L0_xattn_ref(_layernorm(x, axis=-1), ctx_1024, ctx_1024, mask_Bx1xSxS2_ik1, L0_xattn_Wq, L0_xattn_bq, L0_xattn_Wk, L0_xattn_bk, L0_xattn_Wv, L0_xattn_bv, L0_xattn_Wo, L0_xattn_bo)
    x = x + _L0_ffn_ref(_layernorm(x, axis=-1), L0_ffn_w_router, L0_ffn_gate_up_proj, L0_ffn_down_proj, L0_ffn_w_gate, L0_ffn_w_up, L0_ffn_w_down)
    return x

_drawn_inputs = setup_inputs


def setup_inputs(seed=0):
    import zlib

    import numpy as np

    out = dict(_drawn_inputs(seed))
    spreads = {}
    factors = {'L0_xattn_bq': 8.0,
     'L0_xattn_bk': 8.0,
     'L0_xattn_bv': 5.759,
     'L0_xattn_bo': 6.361,
     'L0_ffn_w_router': 6.727,
     'L0_ffn_gate_up_proj': 6.474,
     'L0_ffn_down_proj': 6.462,
     'L0_ffn_w_gate': 2.747,
     'L0_ffn_w_up': 2.697,
     'L0_ffn_w_down': 2.694}
    for name, (base, spread) in spreads.items():
        noise = np.random.default_rng([zlib.crc32(name.encode()), seed]).standard_normal(out[name].shape)
        drawn = base * np.exp(spread * noise) if base else spread * noise
        out[name] = jnp.asarray(drawn.astype(out[name].dtype))
    for name, factor in factors.items():
        out[name] = (out[name] * factor).astype(out[name].dtype)
    return out
```

```python
from contextlib import ExitStack

import concourse.bass as bass
from concourse import mybir

F32 = mybir.dt.float32
I32 = mybir.dt.int32
ALU = mybir.AluOpType
ACT = mybir.ActivationFunctionType
AX_X = mybir.AxisListType.X

P = 128
EPS = 1e-5
MASKED = -1000000000.0
NBUF = 4


def xattn_moe(nc, x, ctxT, mask, wqkvoT, qkbias, vobias, wrT, wguT, wdT, wexp, out):
    B, S, D = x.shape
    K = ctxT.shape[3]
    DC = D // P
    QT = S // P
    T = B * S
    NTT = T // P
    H = 16
    HD = D // H
    HC = H // DC
    HG = HC // 2
    V1 = HD + 1
    SCALE = HD ** -0.5
    E = wrT.shape[2]
    FF = wdT.shape[1] * P
    FC = FF // P
    NT = NTT + E - 1
    UB = QT * DC
    NU = B * UB
    assert UB == 4 and DC == 2 and QT == 2 and E == 16 and NTT == 16 and FC == 4 and B == 8

    ctx = ExitStack()
    with ctx:
        def sb(name, shape, dt=F32):
            return ctx.enter_context(nc.sbuf_tensor(name, shape, dt))

        def sem(name):
            return ctx.enter_context(nc.semaphore(name))

        slots_in = nc.dram_tensor("slots_in", [NT * P, D], F32, kind="Internal").ap()
        slots_out = nc.dram_tensor("slots_out", [NT * P, D], F32, kind="Internal").ap()

        ps = ctx.enter_context(nc.psum_tensor("ps", [P, 8, 512], F32))
        bank_pt, bank_o, bank_m = (4, 5), 6, 7
        bank_g, bank_u, bank_d, bank_x = (0, 1), (2, 3), (4, 5), (6, 7)
        bank_cnt, bank_l = 4, 5

        ident = sb("ident", [P, P])
        ones = sb("ones", [P, P])
        before = sb("before", [P, P])
        headblk = sb("headblk", [P, HC])
        neghalf = sb("neghalf", [P, NTT])
        masked_val = sb("masked_val", [P, 1])
        carrier = sb("carrier", [1, 1])
        zeros = sb("zeros", [P, D])
        rank_rev = sb("rank_rev", [P, E])
        tile_lo = sb("tile_lo", [P, NTT])
        tile_no = sb("tile_no", [1, NT])
        w_qkvo = sb("w_qkvo", [P, 4, DC, D])
        b_qk = sb("b_qk", [P, 2, DC])
        bq_scaled = sb("bq_scaled", [P, DC])
        b_vo = sb("b_vo", [P, 2, D])
        w_r = sb("w_r", [P, DC, E])
        w_gu = sb("w_gu", [P, DC, 2 * FF])
        w_d = sb("w_d", [P, FC, D])

        x_in = [sb(f"x_in{s}", [P, QT, D]) for s in range(2)]
        ctx_in = [sb(f"ctx_in{s}", [P, DC, K]) for s in range(2)]
        mask_in = [sb(f"mask_in{s}", [P, QT, K], I32) for s in range(2)]
        hidden = [sb(f"hidden{s}", [P, QT, K], I32) for s in range(2)]
        bn6 = sb("bn6", [P, QT, 6])
        mv = sb("mv", [P, QT, 2])
        var_eps = sb("var_eps", [P, QT])
        rstd = sb("rstd", [P, QT])
        xn = sb("xn", [P, QT, D])
        xnT = sb("xnT", [P, DC, S])
        qT = [sb(f"qT{s}", [P, DC, S]) for s in range(2)]
        kT = sb("kT", [P, DC, K])
        kblk = [sb(f"kblk{s}", [P, DC, HC, K]) for s in range(2)]
        vals = [sb(f"vals{s}", [K, H, V1]) for s in range(2)]
        prob = [sb(f"prob{s}", [P, HC, K]) for s in range(2)]
        top = sb("top", [P, HC])
        probT = [sb(f"probT{s}", [K, HC, P]) for s in range(2)]
        rden = sb("rden", [P, H])
        att = sb("att", [P, QT, D])
        attT = sb("attT", [P, DC, S])

        x1 = sb("x1", [P, NTT, D])
        bn6b = sb("bn6b", [P, QT, 6])
        mvb = sb("mvb", [P, QT, 2])
        mv2 = sb("mv2", [P, NTT, 2])
        var_eps2 = sb("var_eps2", [P, NTT])
        rstd2 = sb("rstd2", [P, NTT])
        xn2 = sb("xn2", [P, NTT, D])
        xn2T = sb("xn2T", [P, DC, T])

        logits = sb("logits", [P, NTT, E])
        top_l = sb("top_l", [P, NTT])
        pick = sb("pick", [P, NTT, E])
        top_w = sb("top_w", [P, NTT])
        onehot = sb("onehot", [P, NTT, E])
        eneg = sb("eneg", [P, NTT])
        eneg1 = sb("eneg1", [P, NTT])
        score = sb("score", [P, NTT])
        tot = sb("tot", [P, E, NTT])
        upto = sb("upto", [P, E, NTT])
        prev = sb("prev", [P, E, NTT])
        n_e = sb("n_e", [P, E])
        over = sb("over", [P, E, NTT])
        tiles_e = sb("tiles_e", [P, E])
        upto_e = sb("upto_e", [P, E])
        prev_e = sb("prev_e", [P, E])
        adj = sb("adj", [P, E])
        off = sb("off", [P, NTT, E])
        slot_f = sb("slot_f", [P, NTT])
        slot = sb("slot", [P, NTT], I32)
        le = sb("le", [1, NT, E])
        tile_e_f = sb("tile_e_f", [1, NT])
        tile_w = sb("tile_w", [1, NT], I32)

        act_g = [sb(f"act_g{s}", [P, 512]) for s in range(2)]
        hT = [sb(f"hT{s}", [P, FC, S]) for s in range(2)]
        w_e = [sb(f"w_e{s}", [P, DC * 2 * FF + FC * D]) for s in range(NBUF)]
        xs = [sb(f"xs{s}", [P, D]) for s in range(NBUF)]
        xsT = [sb(f"xsT{s}", [P, DC, P]) for s in range(2)]
        ys = [sb(f"ys{s}", [P, D]) for s in range(2)]

        w_attn_in, w_attn_rest_in, w_ffn_in = sem("w_attn_in"), sem("w_attn_rest_in"), sem("w_ffn_in")
        in_ready = [sem(f"in_ready{s}") for s in range(2)]
        const_base, const_ready, bq_ready, const_dve = sem("const_base"), sem("const_ready"), sem("bq_ready"), sem("const_dve")
        ln_step, ve_ready, rstd_ready, xn_ready = sem("ln_step"), sem("ve_ready"), sem("rstd_ready"), sem("xn_ready")
        xres_ready, hidden_ready = sem("xres_ready"), sem("hidden_ready")
        kv_psum, kv_out, kblk_ready = sem("kv_psum"), sem("kv_out"), sem("kblk_ready")
        xnT_psum, xnT_out, q_psum, q_out = sem("xnT_psum"), sem("xnT_out"), sem("q_psum"), sem("q_out")
        s_psum, s_masked, s_top, s_shifted = sem("s_psum"), sem("s_masked"), sem("s_top"), sem("s_shifted")
        exp_done, pt_psum, pt_out, pv_done = sem("exp_done"), sem("pt_psum"), sem("pt_out"), sem("pv_done")
        rden_ready, att_ready = sem("rden_ready"), sem("att_ready")
        attT_psum, attT_out, y_psum, x1_added = sem("attT_psum"), sem("attT_out"), sem("y_psum"), sem("x1_added")
        ln2_step, ve2_ready, rstd2_ready, xn2_ready = sem("ln2_step"), sem("ve2_ready"), sem("rstd2_ready"), sem("xn2_ready")
        xn2T_psum, xn2T_out, l_psum = sem("xn2T_psum"), sem("xn2T_out"), sem("l_psum")
        route_step, top_ready, eneg_ready, onehot_ready = sem("route_step"), sem("top_ready"), sem("eneg_ready"), sem("onehot_ready")
        xs_ready, cnt_psum, slot_ready, tile_e_ready = sem("xs_ready"), sem("cnt_psum"), sem("slot_ready"), sem("tile_e_ready")
        zero_ready, slots_zeroed, scattered = sem("zero_ready"), sem("slots_zeroed"), sem("scattered")
        gu_psum, silu_done, h_ready, d_psum, shared_added = sem("gu_psum"), sem("silu_done"), sem("h_ready"), sem("d_psum"), sem("shared_added")
        we_in = [sem(f"we_in{s}") for s in range(NBUF)]
        xs_in = [sem(f"xs_in{s}") for s in range(NBUF)]
        xsT_psum, xsT_out, egu_psum, esilu_done = sem("xsT_psum"), sem("xsT_out"), sem("egu_psum"), sem("esilu_done")
        eh_ready, ed_psum, ys_ready = sem("eh_ready"), sem("ed_psum"), sem("ys_ready")
        ys_out = [sem(f"ys_out{s}") for s in range(2)]
        gathered = [sem(f"gathered{g}") for g in range(B)]
        out_ready, out_done = sem("out_ready"), sem("out_done")

        block = ctx.enter_context(nc.Block())

        def score_view(s):
            return ps[:, 2 * s:2 * s + 2, 0:HG * K].rearrange("p g (h k) -> p g h k", h=HG)

        def batches(eng, body):
            body(0, 0, True, False)
            with eng.Fori(0, B // 2 - 1) as i:
                body(i, 1, False, False)
                body(i + 1, 0, False, False)
            body(B // 2 - 1, 1, False, True)

        def groups(eng, body):
            batches(eng, body)

        def slot_tiles(eng, body):
            body(0, 0, True, False)
            with eng.Fori(0, (NT - 1) // NBUF) as i:
                for r in range(1, NBUF + 1):
                    body(i + r // NBUF, r % NBUF, False, False)
            left = (NT - 1) % NBUF
            for r in range(1, left + 1):
                body((NT - 1) // NBUF, r, False, r == left)

        @block.sync
        def _(sp):
            def load_batch(b):
                s = b % 2
                sp.dma_start(ctx_in[s][:, :, :], ctxT[b]).then_inc(in_ready[s], 16)
                sp.dma_start(x_in[s][:, :, :], x[b].rearrange("(t p) d -> p t d", p=P)).then_inc(in_ready[s], 16)
                sp.dma_start(mask_in[s][:, :, :], mask[b, 0].rearrange("(t p) k -> p t k", p=P)).then_inc(in_ready[s], 16)

            load_batch(0)
            sp.dma_start(w_qkvo[:, 0:3], wqkvoT[:, 0:3]).then_inc(w_attn_in, 16)
            sp.dma_start(b_qk[:, :, :], qkbias).then_inc(w_attn_in, 16)
            sp.dma_start(b_vo[:, :, :], vobias.rearrange("(o a) d -> o a d", o=1).to_broadcast([P, 2, D])).then_inc(w_attn_in, 16)
            load_batch(1)
            sp.dma_start(w_qkvo[:, 3:4], wqkvoT[:, 3:4]).then_inc(w_attn_rest_in, 16)
            sp.dma_start(w_r[:, :, :], wrT).then_inc(w_ffn_in, 16)
            sp.dma_start(w_gu[:, :, :], wguT).then_inc(w_ffn_in, 16)
            sp.dma_start(w_d[:, :, :], wdT).then_inc(w_ffn_in, 16)
            sp.wait_ge(zero_ready, 1)
            sp.dma_start(slots_in.rearrange("(j p) d -> p j d", p=P),
                         zeros[:, :].rearrange("p (o d) -> p o d", o=1).to_broadcast([P, NT, D])).then_inc(slots_zeroed, 16)

            for b in range(B - 2):
                sp.wait_ge(kv_psum, b + 1)
                sp.wait_ge(xn_ready, 2 * (b + 1))
                sp.wait_ge(xres_ready, b + 1)
                sp.wait_ge(hidden_ready, b + 1)
                load_batch(b + 2)

            sp.wait_ge(tile_e_ready, 1)

            w_size = P * wexp.shape[2]
            experts = wexp.rearrange("e p n -> (e p n)")

            def load_rows(j, s):
                sp.dma_start(xs[s][:, :], slots_in[bass.ds(j * P, P)]).then_inc(xs_in[s], 16)

            def load_weights(at, s):
                sp.dma_start(w_e[s][:, :], experts[bass.ds(at, w_size)].rearrange("(p n) -> p n", p=P)).then_inc(we_in[s], 16)

            def load_tile(j, s):
                at = sp.value_load(tile_w[0:1, bass.ds(j, 1)], min_val=0, max_val=(E - 1) * w_size)
                sp.wait_ge(ed_psum, j + (1 - NBUF))
                load_rows(j, s)
                load_weights(at, s)

            for j in range(NBUF):
                load_weights(sp.value_load(tile_w[0:1, j:j + 1], min_val=0, max_val=(E - 1) * w_size), j)
            sp.wait_ge(scattered, 16 * NTT)
            for j in range(NBUF):
                load_rows(j, j)
            full = (NT - NBUF) // NBUF
            with sp.Fori(0, full) as i:
                for s in range(NBUF):
                    load_tile(NBUF * i + (NBUF + s), s)
            for s in range((NT - NBUF) % NBUF):
                load_tile(NBUF * (full + 1) + s, s)

            for g in range(B):
                sp.wait_ge(out_ready, QT * (g + 1))
                sp.dma_start(out[g].rearrange("(t p) d -> p t d", p=P), x1[:, QT * g:QT * (g + 1), :]).then_inc(out_done, 16)
            sp.wait_ge(out_done, 16 * B)

        @block.gpsimd
        def _(pool):
            pool.memset(zeros[:, :], 0.0).then_inc(zero_ready, 1)
            pool.memset(ident[:, :], 0.0).then_inc(const_base, 1)
            pool.memset(ones[:, :], 1.0).then_inc(const_base, 1)
            pool.memset(neghalf[:, :], -0.5).then_inc(const_ready, 1)
            pool.memset(masked_val[:, :], MASKED).then_inc(const_ready, 1)
            pool.wait_ge(const_base, 2)
            pool.affine_select(out=ident[:, :], in_=ident[:, :], compare_op=ALU.not_equal, fill=1.0,
                               base=0, pattern=[[-1, P]], channel_multiplier=1).then_inc(const_ready, 1)
            pool.affine_select(out=before[:, :], in_=ones[:, :], compare_op=ALU.is_gt, fill=0.0,
                               base=0, pattern=[[1, P]], channel_multiplier=-1).then_inc(const_ready, 1)
            pool.affine_select(out=headblk[:, :], in_=ones[:, 0:HC], compare_op=ALU.is_ge, fill=0.0,
                               base=0, pattern=[[-HD, HC]], channel_multiplier=1).then_inc(const_base, 1)
            pool.wait_ge(const_base, 3)
            pool.affine_select(out=headblk[:, :], in_=headblk[:, :], compare_op=ALU.is_gt, fill=0.0,
                               base=HD, pattern=[[HD, HC]], channel_multiplier=-1).then_inc(const_ready, 1)
            pool.iota(rank_rev[:, :], pattern=[[-1, E]], base=E, channel_multiplier=0,
                      allow_small_or_imprecise_dtypes=True).then_inc(const_ready, 1)
            pool.iota(tile_lo[:, :], pattern=[[P, NTT]], base=0, channel_multiplier=0,
                      allow_small_or_imprecise_dtypes=True).then_inc(const_ready, 1)
            pool.iota(tile_no[:, :], pattern=[[1, NT]], base=0, channel_multiplier=0,
                      allow_small_or_imprecise_dtypes=True).then_inc(const_ready, 1)
            for s in range(2):
                pool.memset(vals[s][:, :, HD:V1], 1.0).then_inc(const_ready, 1)
            pool.wait_ge(w_attn_in, 48)
            pool.wait_ge(const_ready, 10)
            pool.tensor_scalar(bq_scaled[:, :], b_qk[:, 0, :], SCALE, None, ALU.mult).then_inc(bq_ready, 1)

            def prepare(q, s, wait_old):
                b = 2 * q + s
                pool.wait_ge(ve_ready, b + 1)
                pool.tensor_tensor(rstd[:, :], var_eps[:, :], neghalf[:, 0:QT], ALU.pow).then_inc(rstd_ready, 1)
                pool.tensor_tensor(x1[:, bass.ds(QT * b, QT), :], x_in[s][:, :, :],
                                   b_vo[:, 1:2, :].to_broadcast([P, QT, D]), ALU.add).then_inc(xres_ready, 1)
                pool.wait_ge(kv_out, 3 * (b + 1))
                for c in range(DC):
                    pool.tensor_tensor(kblk[s][:, c], kT[:, c:c + 1, :].to_broadcast([P, HC, K]),
                                       headblk[:, :].rearrange("p (h o) -> p h o", o=1).to_broadcast([P, HC, K]),
                                       ALU.mult).then_inc(kblk_ready, 1)

            prepare(0, 0, False)
            prepare(0, 1, True)
            with pool.Fori(0, B // 2 - 1) as i:
                prepare(i + 1, 0, True)
                prepare(i + 1, 1, True)

            pool.wait_ge(ve2_ready, 1)
            pool.tensor_tensor(rstd2[:, :], var_eps2[:, :], neghalf[:, :], ALU.pow).then_inc(rstd2_ready, 1)

            pool.wait_ge(slot_ready, 1)
            pool.wait_ge(slots_zeroed, 16)
            pool.wait_ge(xs_ready, NTT)
            for t in range(NTT):
                pool.indirect_dma_start(slots_in, bass.IndirectOffsetOnAxis(ap=slot[:, t:t + 1], axis=0),
                                        xn2[:, t, :], None).then_inc(scattered, 16)

            def store(q, s, first, last):
                j = NBUF * q + s
                pool.wait_ge(ys_ready, j + 1)
                pool.wait_ge(const_ready, 10)
                pool.dma_start(slots_out[bass.ds(j * P, P)], ys[s % 2][:, :]).then_inc(ys_out[s % 2], 16)

            slot_tiles(pool, store)
            pool.wait_ge(ys_out[0], 16 * ((NT + 1) // 2))
            pool.wait_ge(ys_out[1], 16 * (NT // 2))
            for t in range(NTT):
                pool.indirect_dma_start(xn2[:, t, :], None, slots_out,
                                        bass.IndirectOffsetOnAxis(ap=slot[:, t:t + 1], axis=0)).then_inc(gathered[t // QT], 16)

        @block.tensor
        def _(pe):
            def project_kv(q, s, first, started):
                b = 2 * q + s
                pe.wait_ge(in_ready[s], 48 * (q + 1))
                if started:
                    pe.wait_ge(x1_added, b - 2)
                for c in range(DC):
                    for k in range(DC):
                        pe.matmul(ps[:, bank_m, c * K:(c + 1) * K], w_qkvo[:, 1, k, c * P:(c + 1) * P],
                                  ctx_in[s][:, k, :], start=(k == 0), stop=(k == DC - 1))
                for k in range(DC):
                    mm = pe.matmul(ps[0:K, bank_m, 2 * K:2 * K + D], ctx_in[s][:, k, :], w_qkvo[:, 2, k, :],
                                   start=(k == 0), stop=(k == DC - 1))
                mm.then_inc(kv_psum, 1)

            def transpose_xn(q, s):
                b = 2 * q + s
                pe.wait_ge(xn_ready, 2 * (b + 1))
                pe.wait_ge(kv_out, 3 * (b + 1))
                for c in range(DC):
                    for t in range(QT):
                        mm = pe.transpose(ps[:, bank_m, c * S + t * P:c * S + (t + 1) * P],
                                          xn[:, t, c * P:(c + 1) * P], ident[:, :])
                mm.then_inc(xnT_psum, 1)

            def project_q(q, s, after_attT):
                b = 2 * q + s
                pe.wait_ge(xnT_out, b + 1)
                if after_attT:
                    pe.wait_ge(attT_out, b - 1)
                for c in range(DC):
                    for k in range(DC):
                        mm = pe.matmul(ps[:, bank_m, c * S:(c + 1) * S], w_qkvo[:, 0, k, c * P:(c + 1) * P],
                                       xnT[:, k, :], start=(k == 0), stop=(k == DC - 1))
                mm.then_inc(q_psum, 1)

            def scores(q, s, k, started):
                b = 2 * q + s
                u = UB * b + k
                t, c = k // DC, k % DC
                if k == 0:
                    pe.wait_ge(q_out, DC * (b + 1))
                    pe.wait_ge(kblk_ready, DC * (b + 1))
                if started:
                    pe.wait_ge(s_shifted, u - 1)
                for g in range(2):
                    mm = pe.matmul(ps[:, 2 * (k % 2) + g, 0:HG * K], qT[s][:, c, t * P:(t + 1) * P],
                                   kblk[s][:, c, g * HG:(g + 1) * HG, :].rearrange("p h k -> p (h k)"), start=True, stop=True)
                mm.then_inc(s_psum, 1)

            def transpose_prob(q, s, k, first):
                u = UB * (2 * q + s) + k
                pe.wait_ge(exp_done, u + 1)
                for g in range(2):
                    if not (first and k == 0):
                        pe.wait_ge(pt_out, 2 * u - 1 + g)
                    for h in range(HG):
                        mm = pe.transpose(ps[0:K, bank_pt[g], h * P:(h + 1) * P], prob[k % 2][:, g * HG + h, :], ident[:, :])
                    mm.then_inc(pt_psum, 1)

            def attend(q, s, k, started):
                b = 2 * q + s
                u = UB * b + k
                c = k % DC
                pe.wait_ge(pt_out, 2 * (u + 1))
                if c == 0 and started:
                    pe.wait_ge(att_ready, QT * b + k // DC)
                for h in range(HC):
                    mm = pe.matmul(ps[:, bank_o, (c * HC + h) * V1:(c * HC + h + 1) * V1], probT[k % 2][:, h, :],
                                   vals[s][:, c * HC + h, :], start=True, stop=True)
                mm.then_inc(pv_done, 1)

            def transpose_att(q, s):
                b = 2 * q + s
                pe.wait_ge(att_ready, QT * (b + 1))
                for c in range(DC):
                    for t in range(QT):
                        mm = pe.transpose(ps[:, bank_m, c * S + t * P:c * S + (t + 1) * P],
                                          att[:, t, c * P:(c + 1) * P], ident[:, :])
                mm.then_inc(attT_psum, 1)

            def project_out(q, s):
                b = 2 * q + s
                pe.wait_ge(attT_out, b + 1)
                for t in range(QT):
                    for k in range(DC):
                        mm = pe.matmul(ps[:, bank_m, t * D:(t + 1) * D], attT[:, k, t * P:(t + 1) * P], w_qkvo[:, 3, k, :],
                                       start=(k == 0), stop=(k == DC - 1))
                mm.then_inc(y_psum, 1)

            def before_(q, s):
                return (q, 0) if s else (q - 1, 1)

            def after_(q, s):
                return (q + 1, 0) if s else (q, 1)

            def batch(q, s, first, last):
                b = 2 * q + s
                nq, ns = after_(q, s)
                scores(q, s, 1, not first)
                if not first:
                    attend(*before_(q, s), UB - 1, True)
                if not last:
                    project_kv(nq, ns, False, not first)
                transpose_prob(q, s, 0, first)
                scores(q, s, 2, True)
                attend(q, s, 0, not first)
                if not last:
                    transpose_xn(nq, ns)
                transpose_prob(q, s, 1, False)
                if not first:
                    if not last:
                        pe.wait_ge(xnT_out, b + 2)
                    else:
                        pe.wait_ge(x1_added, b - 1)
                    transpose_att(*before_(q, s))
                scores(q, s, 3, True)
                attend(q, s, 1, True)
                if not last:
                    project_q(nq, ns, not first)
                transpose_prob(q, s, 2, False)
                if not first:
                    if not last:
                        pe.wait_ge(q_out, DC * (b + 2))
                    project_out(*before_(q, s))
                if not last:
                    scores(nq, ns, 0, True)
                attend(q, s, 2, True)
                transpose_prob(q, s, 3, False)

            pe.wait_ge(w_attn_in, 48)
            project_kv(0, 0, True, False)
            pe.wait_ge(const_ready, 10)
            transpose_xn(0, 0)
            project_q(0, 0, False)
            scores(0, 0, 0, False)
            pe.wait_ge(w_attn_rest_in, 16)
            batches(pe, batch)
            attend(B // 2 - 1, 1, UB - 1, True)
            pe.wait_ge(x1_added, B - 1)
            transpose_att(B // 2 - 1, 1)
            project_out(B // 2 - 1, 1)

            pe.wait_ge(w_ffn_in, 48)
            for g in range(B):
                pe.wait_ge(xn2_ready, QT * (g + 1))
                if g == 0:
                    pe.wait_ge(x1_added, B)
                    pe.wait_ge(att_ready, NTT)
                if g >= 2:
                    pe.wait_ge(xn2T_out, g - 1)
                for c in range(DC):
                    for t in range(QT):
                        mm = pe.transpose(ps[:, bank_x[g % 2], c * S + t * P:c * S + (t + 1) * P],
                                          xn2[:, QT * g + t, c * P:(c + 1) * P], ident[:, :])
                mm.then_inc(xn2T_psum, 1)
                if g >= 1:
                    router_logits = g - 1
                    pe.wait_ge(xn2T_out, g)
                    for t in range(QT * router_logits, QT * g):
                        for k in range(DC):
                            pe.matmul(ps[:, bank_l, t * E:(t + 1) * E], xn2T[:, k, t * P:(t + 1) * P], w_r[:, k, :],
                                      start=(k == 0), stop=(k == DC - 1))
            pe.wait_ge(xn2T_out, B)
            for t in range(QT * (B - 1), NTT):
                for k in range(DC):
                    mm = pe.matmul(ps[:, bank_l, t * E:(t + 1) * E], xn2T[:, k, t * P:(t + 1) * P], w_r[:, k, :],
                                   start=(k == 0), stop=(k == DC - 1))
            mm.then_inc(l_psum, 1)

            def gate_up(g, n, first):
                if not first:
                    pe.wait_ge(h_ready, 2 * g - 1 + n)
                for part, bank in ((0, bank_g[n]), (1, bank_u[n])):
                    for m in range(2):
                        col = part * FF + (2 * n + m) * P
                        for k in range(DC):
                            mm = pe.matmul(ps[:, bank, m * S:(m + 1) * S], w_gu[:, k, col:col + P],
                                           xn2T[:, k, bass.ds(g * S, S)], start=(k == 0), stop=(k == DC - 1))
                    mm.then_inc(gu_psum, 1)

            def down(g, s, first):
                pe.wait_ge(h_ready, 2 * (g + 1))
                if not first:
                    pe.wait_ge(shared_added, g - 1)
                for t in range(QT):
                    for k in range(FC):
                        mm = pe.matmul(ps[:, bank_d[s], t * D:(t + 1) * D], hT[s][:, k, t * P:(t + 1) * P], w_d[:, k, :],
                                       start=(k == 0), stop=(k == FC - 1))
                mm.then_inc(d_psum, 1)

            gate_up(0, 0, True)
            gate_up(0, 1, True)
            pe.wait_ge(onehot_ready, 1)
            oh = onehot[:, :, :].rearrange("p t e -> p (t e)")
            pe.matmul(ps[:, bank_cnt, 0:NTT * E], before[:, :], oh, start=True, stop=True)
            pe.matmul(ps[:, bank_cnt, NTT * E:2 * NTT * E], ones[:, :], oh, start=True, stop=True).then_inc(cnt_psum, 1)

            def group(q, s, first, last):
                g = 2 * q + s
                if not first:
                    gate_up(g, 0, False)
                    if s == 1:
                        down(g - 1, 0, False)
                    else:
                        down(g - 1, 1, False)
                    gate_up(g, 1, False)

            gate_up(1, 0, False)
            pe.wait_ge(slot_ready, 1)
            down(0, 0, True)
            gate_up(1, 1, False)
            gate_up(2, 0, False)
            down(1, 1, True)
            gate_up(2, 1, False)
            with pe.Fori(0, (B - 4) // 2) as i:
                for r in range(2):
                    g = 2 * i + (3 + r)
                    gate_up(g, 0, False)
                    down(g - 1, r % 2, False)
                    gate_up(g, 1, False)
            gate_up(B - 1, 0, False)
            down(B - 2, 0, False)
            gate_up(B - 1, 1, False)
            down(B - 1, 1, False)

            def transpose_rows(j, s, xq, first2):
                pe.wait_ge(xs_in[s], 16 * (xq + 1))
                if not first2:
                    pe.wait_ge(xsT_out, j - 1)
                for c in range(DC):
                    mm = pe.transpose(ps[:, bank_x[s % 2], c * P:(c + 1) * P], xs[s][:, c * P:(c + 1) * P], ident[:, :])
                mm.then_inc(xsT_psum, 1)

            def expert_gate_up(j, s, q, first2):
                pe.wait_ge(we_in[s], 16 * (q + 1))
                pe.wait_ge(xsT_out, j + 1)
                if not first2:
                    pe.wait_ge(eh_ready, j - 1)
                for part, bank in ((0, bank_g[s % 2]), (1, bank_u[s % 2])):
                    for m in range(FC):
                        for k in range(DC):
                            col = k * 2 * FF + part * FF + m * P
                            mm = pe.matmul(ps[:, bank, m * P:(m + 1) * P], w_e[s][:, col:col + P], xsT[s % 2][:, k, :],
                                           start=(k == 0), stop=(k == DC - 1))
                    mm.then_inc(egu_psum, 1)

            def expert_down(j, s, first2):
                pe.wait_ge(eh_ready, j + 1)
                if not first2:
                    pe.wait_ge(ys_ready, j - 1)
                for k in range(FC):
                    col = DC * 2 * FF + k * D
                    mm = pe.matmul(ps[:, bank_d[s % 2], 0:D], hT[s % 2][:, k, 0:P], w_e[s][:, col:col + D],
                                   start=(k == 0), stop=(k == FC - 1))
                mm.then_inc(ed_psum, 1)

            pe.wait_ge(h_ready, 2 * B)
            pe.wait_ge(shared_added, B)

            def tile(q, s, j=None):
                j = NBUF * q + s if j is None else j
                transpose_rows(j, s, q, j in (0, 1) if isinstance(j, int) else False)
                if isinstance(j, int) and j == 0:
                    return
                expert_gate_up(j - 1, (s - 1) % NBUF, q - (s == 0), isinstance(j, int) and j <= 2)
                if isinstance(j, int) and j == 1:
                    return
                expert_down(j - 2, (s - 2) % NBUF, isinstance(j, int) and j <= 3)

            for j in range(NBUF):
                tile(0, j, j)
            rounds = NT // NBUF - 1
            with pe.Fori(1, 1 + rounds) as i:
                for r in range(NBUF):
                    tile(i, r)
            for j in range(NBUF * (1 + rounds), NT):
                tile(j // NBUF, j % NBUF, j)
            expert_gate_up(NT - 1, (NT - 1) % NBUF, (NT - 1) // NBUF, False)
            expert_down(NT - 2, (NT - 2) % NBUF, False)
            expert_down(NT - 1, (NT - 1) % NBUF, False)

        @block.scalar
        def _(act):
            def read_xnT(q, s):
                b = 2 * q + s
                act.wait_ge(xnT_psum, b + 1)
                act.activation(xnT[:, :, :].rearrange("p c n -> p (c n)"), ps[:, bank_m, :], ACT.Copy).then_inc(xnT_out, 1)

            def read_q(q, s):
                b = 2 * q + s
                act.wait_ge(q_psum, b + 1)
                for c in range(DC):
                    act.activation(qT[s][:, c, :], ps[:, bank_m, c * S:(c + 1) * S], ACT.Identity,
                                   bias=bq_scaled[:, c:c + 1], scale=SCALE).then_inc(q_out, 1)

            def read_attT(q, s):
                b = 2 * q + s
                act.wait_ge(attT_psum, b + 1)
                act.activation(attT[:, :, :].rearrange("p c n -> p (c n)"), ps[:, bank_m, :], ACT.Copy).then_inc(attT_out, 1)

            def unit(q, s, k, started):
                u = UB * (2 * q + s) + k
                act.wait_ge(s_shifted, u + 1)
                act.activation(prob[k % 2][:, :, :], prob[k % 2][:, :, :], ACT.Exp).then_inc(exp_done, 1)
                for g in range(2):
                    act.wait_ge(pt_psum, 2 * u + g + 1)
                    if started and g == 0:
                        act.wait_ge(pv_done, u - 1)
                    act.activation(probT[k % 2][:, g * HG:(g + 1) * HG, :].rearrange("p h n -> p (h n)"),
                                   ps[0:K, bank_pt[g], :], ACT.Copy).then_inc(pt_out, 1)

            def batch(q, s, first, last):
                nq, ns = (q + 1, 0) if s else (q, 1)
                pq, pp = (q, 0) if s else (q - 1, 1)
                unit(q, s, 0, not first)
                if not last:
                    read_xnT(nq, ns)
                unit(q, s, 1, not first)
                if not first:
                    read_attT(pq, pp)
                if not last:
                    read_q(nq, ns)
                unit(q, s, 2, True)
                unit(q, s, 3, True)

            act.wait_ge(bq_ready, 1)
            read_xnT(0, 0)
            read_q(0, 0)
            batches(act, batch)
            read_attT(B // 2 - 1, 1)

            for g in range(B):
                act.wait_ge(xn2T_psum, g + 1)
                act.activation(xn2T[:, :, g * S:(g + 1) * S], ps[:, bank_x[g % 2], :].rearrange("p (c n) -> p c n", c=DC),
                               ACT.Copy).then_inc(xn2T_out, 1)
            act.wait_ge(top_ready, 1)
            act.activation(eneg[:, :], top_l[:, :], ACT.Exp, scale=-1.0).then_inc(eneg_ready, 1)

            def silu(g, n, started):
                act.wait_ge(gu_psum, 4 * g + 2 * n + 1)
                if started:
                    act.wait_ge(h_ready, 2 * g - 1 + n)
                act.activation(act_g[n][:, :], ps[:, bank_g[n], :], ACT.Silu).then_inc(silu_done, 1)

            silu(0, 0, False)
            silu(0, 1, False)
            with act.Fori(1, B) as g:
                silu(g, 0, True)
                silu(g, 1, True)

            def tile(q, s, first, last):
                j = NBUF * q + s
                act.wait_ge(xsT_psum, j + 1)
                act.activation(xsT[s % 2][:, :, :].rearrange("p c n -> p (c n)"), ps[:, bank_x[s % 2], 0:DC * P],
                               ACT.Copy).then_inc(xsT_out, 1)
                if not first:
                    gate(j - 1, (s - 1) % 2)

            def gate(j, s):
                act.wait_ge(egu_psum, 2 * j + 1)
                act.activation(act_g[s][:, :], ps[:, bank_g[s], :], ACT.Silu).then_inc(esilu_done, 1)

            act.wait_ge(h_ready, 2 * B)
            slot_tiles(act, tile)
            gate(NT - 1, (NT - 1) % 2)

        @block.vector
        def _(dve):
            def apart():
                dve.memset(carrier[:, :], 0.0)

            def ln1_stats(q, s):
                b = 2 * q + s
                dve.wait_ge(in_ready[s], 48 * (q + 1))
                for t in range(QT):
                    dve.bn_stats(bn6[:, t, :], x_in[s][:, t, :]).then_inc(ln_step, 1)
                dve.wait_ge(ln_step, 4 * b + 2)
                apart()
                for t in range(QT):
                    dve.bn_aggr(mv[:, t, :], bn6[:, t, :]).then_inc(ln_step, 1)
                dve.wait_ge(ln_step, 4 * b + 4)
                dve.tensor_scalar(var_eps[:, :], mv[:, :, 1], EPS, None, ALU.add).then_inc(ve_ready, 1)

            def ln1_apply(q, s, started):
                b = 2 * q + s
                dve.wait_ge(rstd_ready, b + 1)
                if started:
                    dve.wait_ge(xnT_psum, b)
                for t in range(QT):
                    dve.tensor_scalar(xn[:, t, :], x_in[s][:, t, :], mv[:, t, 0:1], rstd[:, t:t + 1],
                                      ALU.subtract, ALU.mult).then_inc(xn_ready, 1)

            def turn_mask(q, s):
                dve.tensor_scalar(hidden[s][:, :, :], mask_in[s][:, :, :], 0.0, None, ALU.is_equal).then_inc(hidden_ready, 1)

            def read_kv(q, s, started):
                b = 2 * q + s
                dve.wait_ge(kv_psum, b + 1)
                if started:
                    dve.wait_ge(kblk_ready, DC * b)
                for c in range(DC):
                    dve.tensor_scalar(kT[:, c, :], ps[:, bank_m, c * K:(c + 1) * K], b_qk[:, 1, c:c + 1], None,
                                      ALU.add).then_inc(kv_out, 1)
                dve.tensor_tensor(vals[s][:, :, 0:HD], ps[0:K, bank_m, 2 * K:2 * K + D].rearrange("k (h d) -> k h d", h=H),
                                  b_vo[0:K, 0, :].rearrange("k (h d) -> k h d", h=H), ALU.add).then_inc(kv_out, 1)

            def softmax_shift(q, s, k, started):
                b = 2 * q + s
                u = UB * b + k
                t = k // DC
                sv = score_view(k % 2)
                dve.wait_ge(s_psum, u + 1)
                if k == 0:
                    dve.wait_ge(hidden_ready, b + 1)
                apart()
                for g in range(2):
                    dve.copy_predicated(sv[:, g], hidden[s][:, t:t + 1, :].to_broadcast([P, HG, K]),
                                        masked_val[:, :].rearrange("p (a o) -> p a o", a=1).to_broadcast([P, HG, K])).then_inc(s_masked, 1)
                dve.wait_ge(s_masked, 2 * (u + 1))
                dve.tensor_reduce(top[:, :].rearrange("p (g h) -> p g h", g=2), sv, AX_X, ALU.max).then_inc(s_top, 1)
                dve.wait_ge(s_top, u + 1)
                if started:
                    dve.wait_ge(pt_psum, 2 * (u - 1))
                dve.tensor_tensor(prob[k % 2][:, :, :].rearrange("p (g h) k -> p g h k", g=2), sv,
                                  top[:, :].rearrange("p (g h o) -> p g h o", g=2, o=1).to_broadcast([P, 2, HG, K]),
                                  ALU.subtract).then_inc(s_shifted, 1)

            def normalise(q, s, t):
                b = 2 * q + s
                n = QT * b + t
                o = ps[:, bank_o, 0:H * V1].rearrange("p (h v) -> p h v", h=H)
                dve.wait_ge(pv_done, DC * (n + 1))
                dve.reciprocal(rden[:, :], o[:, :, HD]).then_inc(rden_ready, 1)
                dve.wait_ge(rden_ready, n + 1)
                dve.tensor_tensor(att[:, t, :].rearrange("p (h d) -> p h d", h=H), o[:, :, 0:HD],
                                  rden[:, :].rearrange("p (h o) -> p h o", o=1).to_broadcast([P, H, HD]),
                                  ALU.mult).then_inc(att_ready, 1)

            def add_attention(q, s):
                b = 2 * q + s
                dve.wait_ge(y_psum, b + 1)
                dve.wait_ge(xres_ready, b + 1)
                here = x1[:, bass.ds(QT * b, QT), :]
                dve.tensor_tensor(here, ps[:, bank_m, :].rearrange("p (t d) -> p t d", t=QT), here, ALU.add).then_inc(x1_added, 1)
                dve.wait_ge(x1_added, b + 1)
                apart()
                for t in range(QT):
                    dve.bn_stats(bn6b[:, t, :], x1[:, bass.ds(QT * b + t, 1), :].rearrange("p o d -> p (o d)")).then_inc(ln2_step, 1)
                dve.wait_ge(ln2_step, 5 * b + 2)
                apart()
                for t in range(QT):
                    dve.bn_aggr(mvb[:, t, :], bn6b[:, t, :]).then_inc(ln2_step, 1)
                dve.wait_ge(ln2_step, 5 * b + 4)
                dve.tensor_copy(mv2[:, bass.ds(QT * b, QT), :], mvb[:, :, :]).then_inc(ln2_step, 1)

            def batch(q, s, first, last):
                nq, ns = (q + 1, 0) if s else (q, 1)
                pq, pp = (q, 0) if s else (q - 1, 1)
                if not last:
                    ln1_stats(nq, ns)
                softmax_shift(q, s, 0, not first)
                if not first:
                    normalise(pq, pp, 1)
                if not last:
                    turn_mask(nq, ns)
                    read_kv(nq, ns, True)
                    ln1_apply(nq, ns, True)
                softmax_shift(q, s, 1, not first)
                softmax_shift(q, s, 2, True)
                normalise(q, s, 0)
                softmax_shift(q, s, 3, True)
                if not first:
                    add_attention(pq, pp)

            dve.wait_ge(w_attn_in, 48)
            dve.wait_ge(const_ready, 10)
            ln1_stats(0, 0)
            turn_mask(0, 0)
            read_kv(0, 0, False)
            ln1_apply(0, 0, False)
            batches(dve, batch)
            normalise(B // 2 - 1, 1, 1)
            add_attention(B // 2 - 1, 1)

            dve.wait_ge(ln2_step, 5 * B)
            dve.tensor_scalar(var_eps2[:, :], mv2[:, :, 1], EPS, None, ALU.add).then_inc(ve2_ready, 1)
            dve.wait_ge(rstd2_ready, 1)
            for t in range(NTT):
                dve.tensor_scalar(xn2[:, t, :], x1[:, t, :], mv2[:, t, 0:1], rstd2[:, t:t + 1],
                                  ALU.subtract, ALU.mult).then_inc(xn2_ready, 1)

            steps = [0]

            def step(ins):
                ins.then_inc(route_step, 1)
                steps[0] += 1
                dve.wait_ge(route_step, steps[0])

            def over_e(ap):
                return ap.rearrange("p (t o) -> p t o", o=1).to_broadcast([P, NTT, E])

            def over_t(ap):
                return ap.rearrange("p (o e) -> p o e", o=1).to_broadcast([P, NTT, E])

            dve.wait_ge(l_psum, 1)
            lp = ps[:, bank_l, 0:NTT * E].rearrange("p (t e) -> p t e", t=NTT)
            dve.tensor_reduce(top_l[:, :], lp, AX_X, ALU.max).then_inc(top_ready, 1)
            dve.wait_ge(top_ready, 1)
            step(dve.tensor_tensor(pick[:, :, :], lp, over_e(top_l[:, :]), ALU.is_equal))
            step(dve.tensor_tensor(logits[:, :, :], pick[:, :, :], over_t(rank_rev[:, :]), ALU.mult))
            step(dve.tensor_reduce(top_w[:, :], logits[:, :, :], AX_X, ALU.max))
            dve.tensor_tensor(onehot[:, :, :], over_t(rank_rev[:, :]), over_e(top_w[:, :]), ALU.is_equal).then_inc(onehot_ready, 1)
            dve.wait_ge(eneg_ready, 1)
            step(dve.tensor_scalar(eneg1[:, :], eneg[:, :], 1.0, None, ALU.add))
            step(dve.reciprocal(score[:, :], eneg1[:, :]))
            dve.wait_ge(xn2T_psum, B)
            for t in range(NTT):
                dve.tensor_scalar(xn2[:, t, :], xn2[:, t, :], score[:, t:t + 1], None, ALU.mult).then_inc(xs_ready, 1)

            def hidden_out(g, n, s):
                dve.wait_ge(silu_done, 2 * g + n + 1)
                dve.wait_ge(gu_psum, 4 * g + 2 * n + 2)
                dve.tensor_tensor(hT[s][:, 2 * n:2 * n + 2, :].rearrange("p m n -> p (m n)"), act_g[n][:, :],
                                  ps[:, bank_u[n], :], ALU.mult).then_inc(h_ready, 1)

            def add_shared(g, s):
                dve.wait_ge(d_psum, g + 1)
                here = x1[:, bass.ds(QT * g, QT), :]
                dve.tensor_tensor(here, ps[:, bank_d[s], :].rearrange("p (t d) -> p t d", t=QT), here, ALU.add).then_inc(shared_added, 1)

            hidden_out(0, 0, 0)
            hidden_out(0, 1, 0)

            dve.wait_ge(cnt_psum, 1)
            cnt = ps[:, bank_cnt, 0:NTT * E].rearrange("p (t e) -> p t e", t=NTT)
            all_ = ps[:, bank_cnt, NTT * E:2 * NTT * E].rearrange("p (t e) -> p e t", t=NTT)
            flat = lambda a: a[:, :, :].rearrange("p e t -> p (e t)")
            step(dve.tensor_copy(tot[:, :, :], all_))
            step(dve.tensor_tensor_scan(flat(upto), ones[:, 0:1].to_broadcast([P, E * NTT]), flat(tot), 0.0, ALU.mult, ALU.add))
            step(dve.tensor_tensor(prev[:, :, :], upto[:, :, :], tot[:, :, :], ALU.subtract))
            step(dve.tensor_reduce(n_e[:, :], tot[:, :, :], AX_X, ALU.add))
            step(dve.tensor_tensor(over[:, :, :], n_e[:, :].rearrange("p (e o) -> p e o", o=1).to_broadcast([P, E, NTT]),
                                   tile_lo[:, :].rearrange("p (o t) -> p o t", o=1).to_broadcast([P, E, NTT]), ALU.is_gt))
            step(dve.tensor_reduce(tiles_e[:, :], over[:, :, :], AX_X, ALU.add))
            step(dve.tensor_tensor_scan(upto_e[:, :], ones[:, 0:E], tiles_e[:, :], 0.0, ALU.mult, ALU.add))
            step(dve.tensor_tensor(le[:, :, :], upto_e[0:1, :].rearrange("p (o e) -> p o e", o=1).to_broadcast([1, NT, E]),
                                   tile_no[:, :].rearrange("p (j o) -> p j o", o=1).to_broadcast([1, NT, E]), ALU.is_le))
            step(dve.tensor_reduce(tile_e_f[:, :], le[:, :, :], AX_X, ALU.add))
            dve.tensor_scalar(tile_w[:, :], tile_e_f[:, :], float(E - 1), float(P * wexp.shape[2]), ALU.min, ALU.mult).then_inc(tile_e_ready, 1)
            step(dve.tensor_tensor(prev_e[:, :], upto_e[:, :], tiles_e[:, :], ALU.subtract))
            step(dve.scalar_tensor_tensor(adj[:, :], prev_e[:, :], float(P), prev[:, :, 0], ALU.mult, ALU.subtract))
            step(dve.tensor_tensor(off[:, :, :], cnt, prev[:, :, :].rearrange("p e t -> p t e"), ALU.add))
            step(dve.tensor_tensor(pick[:, :, :], off[:, :, :], over_t(adj[:, :]), ALU.add))
            step(dve.tensor_tensor(off[:, :, :], pick[:, :, :], onehot[:, :, :], ALU.mult))
            step(dve.tensor_reduce(slot_f[:, :], off[:, :, :], AX_X, ALU.add))
            dve.tensor_copy(slot[:, :], slot_f[:, :]).then_inc(slot_ready, 1)

            hidden_out(1, 0, 1)
            hidden_out(1, 1, 1)
            with dve.Fori(0, (B - 2) // 2) as i:
                for r in range(2):
                    g = 2 * i + (2 + r)
                    hidden_out(g, 0, r)
                    add_shared(g - 2, r)
                    hidden_out(g, 1, r)
            add_shared(B - 2, 0)
            add_shared(B - 1, 1)

            def expert_hidden(j, s, first2):
                dve.wait_ge(esilu_done, j + 1)
                dve.wait_ge(egu_psum, 2 * (j + 1))
                dve.tensor_tensor(hT[s % 2][:, :, 0:P], act_g[s % 2][:, :].rearrange("p (m n) -> p m n", m=FC),
                                  ps[:, bank_u[s % 2], :].rearrange("p (m n) -> p m n", m=FC), ALU.mult).then_inc(eh_ready, 1)

            def expert_rows(j, s, stored):
                dve.wait_ge(ed_psum, j + 1)
                if stored is not None:
                    dve.wait_ge(ys_out[s % 2], 16 * stored)
                dve.tensor_copy(ys[s % 2][:, :], ps[:, bank_d[s % 2], 0:D]).then_inc(ys_ready, 1)

            expert_hidden(0, 0, True)
            expert_hidden(1, 1, True)
            expert_rows(0, 0, None)
            expert_hidden(2, 0, False)
            expert_rows(1, 1, None)
            with dve.Fori(0, (NT - 3) // 2) as i:
                for r in range(2):
                    j = 2 * i + (3 + r)
                    expert_hidden(j, 1 - r, False)
                    expert_rows(j - 1, r, i + 1)
            expert_rows(NT - 1, 0, (NT - 1) // 2)

            for g in range(B):
                dve.wait_ge(gathered[g], 16 * QT)
                for t in range(QT * g, QT * (g + 1)):
                    dve.tensor_tensor(x1[:, t, :], x1[:, t, :], xn2[:, t, :], ALU.add).then_inc(out_ready, 1)


_OUT = ((8, 256, 256), "float32")


def _chunked(np, w, p=128):
    *lead, r, c = w.shape
    w = w.reshape(*lead, r // p, p, c)
    return np.ascontiguousarray(np.swapaxes(w, -3, -2))


def kernel(x, ctx_1024, mask_Bx1xSxS2_ik1, L0_xattn_Wq, L0_xattn_bq, L0_xattn_Wk, L0_xattn_bk, L0_xattn_Wv,
           L0_xattn_bv, L0_xattn_Wo, L0_xattn_bo, L0_ffn_w_router, L0_ffn_gate_up_proj, L0_ffn_down_proj,
           L0_ffn_w_gate, L0_ffn_w_up, L0_ffn_w_down):
    import numpy as np
    import concourse.bacc as bacc
    from concourse.bass_utils import run_bass_kernel_spmd

    a = np.asarray
    qkvo = np.stack([_chunked(np, a(w).T) for w in (L0_xattn_Wq, L0_xattn_Wk, L0_xattn_Wv, L0_xattn_Wo)], axis=1)
    gate_up = _chunked(np, a(L0_ffn_gate_up_proj))
    down = _chunked(np, a(L0_ffn_down_proj))
    experts = gate_up.shape[0]
    arrays = {
        "x": a(x),
        "ctxT": _chunked(np, np.swapaxes(a(ctx_1024), 1, 2)),
        "mask": a(mask_Bx1xSxS2_ik1),
        "w_qkvoT": qkvo,
        "qk_bias": np.stack([a(L0_xattn_bq).reshape(2, 128).T, a(L0_xattn_bk).reshape(2, 128).T], axis=1),
        "vo_bias": np.stack([a(L0_xattn_bv), a(L0_xattn_bo)]),
        "w_routerT": _chunked(np, a(L0_ffn_w_router).T),
        "w_gate_upT": _chunked(np, np.concatenate([a(L0_ffn_w_gate), a(L0_ffn_w_up)]).T),
        "w_downT": _chunked(np, a(L0_ffn_w_down).T),
        "w_experts": np.concatenate([gate_up.reshape(experts, 128, -1), down.reshape(experts, 128, -1)], axis=2),
    }
    nc = bacc.Bacc("TRN2", target_bir_lowering=False, num_devices=1)
    args = []
    for name, v in arrays.items():
        v = arrays[name] = np.ascontiguousarray(v)
        args.append(nc.dram_tensor(name, v.shape, mybir.dt.from_np(v.dtype), kind="ExternalInput").ap())
    args.append(nc.dram_tensor("out", _OUT[0], mybir.dt.from_np(np.dtype(_OUT[1])), kind="ExternalOutput").ap())
    xattn_moe(nc, *args)
    r = run_bass_kernel_spmd(nc, [arrays], core_ids=[0])
    return r.results[0]["out"]
```

```python
from contextlib import ExitStack

import concourse.bass as bass
from concourse import mybir

F32 = mybir.dt.float32
F16 = mybir.dt.float16
BF16 = mybir.dt.bfloat16
I32 = mybir.dt.int32
ALU = mybir.AluOpType
ACT = mybir.ActivationFunctionType
AX_X = mybir.AxisListType.X

P = 128
EPS = 1e-5
MASKED = -1000000000.0
VISIBLE = 3e38
T_LAG = 3
V_LAG = 4
NBUF = 4


def xattn_moe(nc, x, ctxT, mask, wqkvoT, qkbias, vobias, wrT, wguT, wdT, wexp, out):
    B, S, D = x.shape
    K = ctxT.shape[3]
    DC = D // P
    QT = S // P
    T = B * S
    NTT = T // P
    H = 16
    HD = D // H
    HC = H // DC
    HU = HC // 2
    VP = 3
    VW = VP * HD + 1
    SCALE = HD ** -0.5
    E = wrT.shape[2]
    FF = wdT.shape[1] * P
    FC = FF // P
    NT = NTT + E - 1
    UB = QT * H // HU
    UT = UB // QT
    assert UB == 8 and DC == 2 and QT == 2 and E == 16 and NTT == 16 and FC == 4 and B == 8

    ctx = ExitStack()
    with ctx:
        def sb(name, shape, dt=F32):
            return ctx.enter_context(nc.sbuf_tensor(name, shape, dt))

        def sem(name):
            return ctx.enter_context(nc.semaphore(name))

        slots_in = nc.dram_tensor("slots_in", [NT * P, D + 1], F32, kind="Internal").ap()
        base = nc.dram_tensor("base", [T, D], F32, kind="Internal").ap()

        ps = ctx.enter_context(nc.psum_tensor("ps", [P, 8, 512], F32))
        bank_s, bank_pt, bank_o, bank_m = (0, 1), (2, 3), (4, 5), (6, 7)
        bank_g, bank_u, bank_d, bank_x = (0, 1), (2, 3), (4, 5), (6, 7)
        bank_cnt, bank_l = 4, 5

        ident = sb("ident", [P, P])
        ones = sb("ones", [P, P])
        before = sb("before", [P, P])
        headblk = sb("headblk", [P, HC])
        neghalf = sb("neghalf", [P, QT])
        ident16 = sb("ident16", [P, P], F16)
        carrier = sb("carrier", [1, 1])
        pool_carrier = sb("pool_carrier", [1, 2])
        no_token = sb("no_token", [P, D + 1])
        rank_rev = sb("rank_rev", [P, E])
        tile_lo = sb("tile_lo", [P, NTT])
        tile_no = sb("tile_no", [1, NT])
        w_qkvo = sb("w_qkvo", [P, 4, DC, D])
        b_qk = sb("b_qk", [P, 2, DC])
        bq_scaled = sb("bq_scaled", [P, DC])
        b_vo = sb("b_vo", [P, 2, D])
        w_r = sb("w_r", [P, DC, E])
        w_gu = sb("w_gu", [P, DC, 2 * FF])
        w_d = sb("w_d", [P, FC, D])

        x_in = [sb(f"x_in{s}", [P, QT, D]) for s in range(2)]
        ctx_in = [sb(f"ctx_in{s}", [P, DC, K]) for s in range(2)]
        mask_in = [sb(f"mask_in{s}", [P, QT, K], I32) for s in range(2)]
        cap = [sb(f"cap{s}", [P, QT, K]) for s in range(2)]
        seen = sb("seen", [P, QT, K])
        bn6 = sb("bn6", [P, QT, 6])
        mv = sb("mv", [P, QT, 2])
        var_eps = sb("var_eps", [P, QT])
        rstd = sb("rstd", [P, QT])
        xn = sb("xn", [P, QT, D])
        xnT = sb("xnT", [P, DC, S])
        qT = [sb(f"qT{s}", [P, DC, S]) for s in range(2)]
        kT = sb("kT", [P, DC, K])
        kblk = [sb(f"kblk{s}", [P, DC, HC, K]) for s in range(2)]
        val = sb("val", [K, D])
        val_left = [sb(f"val_left{i}", [K, D]) for i in range(VP - 2)]
        vals = [sb(f"vals{s}", [K, H, VW], BF16) for s in range(2)]
        prob = [sb(f"prob{s}", [P, HU, K]) for s in range(4)]
        prob_hi = [sb(f"prob_hi{s}", [P, HU, K], F16) for s in range(4)]
        prob_lo = [sb(f"prob_lo{s}", [P, HU, K], F16) for s in range(4)]
        top = [sb(f"top{s}", [P, HU]) for s in range(4)]
        probT = [sb(f"probT{s}", [K, 2, HU, P], F16) for s in range(2)]
        rden = [sb(f"rden{s}", [P, HC]) for s in range(2)]
        att_sum = [sb(f"att_sum{s}", [P, HC, HD]) for s in range(2)]
        att = sb("att", [P, QT, D])
        attT = sb("attT", [P, DC, S])

        x1 = sb("x1", [P, NTT, D])
        bn6b = sb("bn6b", [P, QT, 6])
        mvb = sb("mvb", [P, QT, 2])
        var_eps2 = sb("var_eps2", [P, QT])
        rstd2 = sb("rstd2", [P, QT])
        xn2 = sb("xn2", [P, NTT, D + 1])
        xn2T = sb("xn2T", [P, DC, T])

        logits = sb("logits", [P, NTT, E])
        top_l = sb("top_l", [P, NTT])
        pick = sb("pick", [P, NTT, E])
        top_w = sb("top_w", [P, NTT])
        onehot = sb("onehot", [P, NTT, E])
        eneg = sb("eneg", [P, NTT])
        eneg1 = sb("eneg1", [P, NTT])
        score = sb("score", [P, NTT])
        tot = sb("tot", [P, E, NTT])
        upto = sb("upto", [P, E, NTT])
        prev = sb("prev", [P, E, NTT])
        n_e = sb("n_e", [P, E])
        over = sb("over", [P, E, NTT])
        tiles_e = sb("tiles_e", [P, E])
        upto_e = sb("upto_e", [P, E])
        prev_e = sb("prev_e", [P, E])
        adj = sb("adj", [P, E])
        off = sb("off", [P, NTT, E])
        slot_f = sb("slot_f", [P, NTT])
        slot = sb("slot", [P, NTT], I32)
        le = sb("le", [1, NT, E])
        tile_e_f = sb("tile_e_f", [1, NT])
        tile_w = sb("tile_w", [1, NT], I32)

        act_g = [sb(f"act_g{s}", [P, 512]) for s in range(2)]
        hT = [sb(f"hT{s}", [P, FC, S]) for s in range(2)]
        w_e = [sb(f"w_e{s}", [P, DC * 2 * FF + FC * D]) for s in range(NBUF)]
        xs = [sb(f"xs{s}", [P, D + 1]) for s in range(NBUF)]
        token = [sb(f"token{s}", [P, 1], I32) for s in range(NBUF)]
        xb = [sb(f"xb{s}", [P, D]) for s in range(2)]
        xsT = [sb(f"xsT{s}", [P, DC, P]) for s in range(2)]
        ys = [sb(f"ys{s}", [P, D]) for s in range(2)]

        w_attn_in, w_attn_rest_in, w_ffn_in = sem("w_attn_in"), sem("w_attn_rest_in"), sem("w_ffn_in")
        in_ready = [sem(f"in_ready{s}") for s in range(2)]
        const_base, const_ready, bq_ready, const_dve = sem("const_base"), sem("const_ready"), sem("bq_ready"), sem("const_dve")
        ln_step, ve_ready, rstd_ready, xn_ready = sem("ln_step"), sem("ve_ready"), sem("rstd_ready"), sem("xn_ready")
        xres_ready, seen_ready, cap_ready = sem("xres_ready"), sem("seen_ready"), sem("cap_ready")
        hi_ready, lo_ready, val_ready, val_step, vals_ready, att_summed = (sem(n) for n in (
            "hi_ready", "lo_ready", "val_ready", "val_step", "vals_ready", "att_summed"))
        kv_psum, kv_out, kblk_ready = sem("kv_psum"), sem("kv_out"), sem("kblk_ready")
        xnT_psum, xnT_out, q_psum, q_out = sem("xnT_psum"), sem("xnT_out"), sem("q_psum"), sem("q_out")
        s_psum, s_masked, s_top, s_shifted = sem("s_psum"), sem("s_masked"), sem("s_top"), sem("s_shifted")
        exp_done, pt_psum, pt_out, pv_done = sem("exp_done"), sem("pt_psum"), sem("pt_out"), sem("pv_done")
        rden_ready, att_ready = sem("rden_ready"), sem("att_ready")
        attT_psum, attT_out, y_psum, x1_added = sem("attT_psum"), sem("attT_out"), sem("y_psum"), sem("x1_added")
        ln2_step, ve2_ready, rstd2_ready, xn2_ready = sem("ln2_step"), sem("ve2_ready"), sem("rstd2_ready"), sem("xn2_ready")
        xn2T_psum, xn2T_out, l_psum = sem("xn2T_psum"), sem("xn2T_out"), sem("l_psum")
        route_step, top_ready, eneg_ready, onehot_ready = sem("route_step"), sem("top_ready"), sem("eneg_ready"), sem("onehot_ready")
        xs_ready, cnt_psum, slot_ready, tile_e_ready = sem("xs_ready"), sem("cnt_psum"), sem("slot_ready"), sem("tile_e_ready")
        zero_ready, slots_zeroed, scattered = sem("zero_ready"), sem("slots_zeroed"), sem("scattered")
        gu_psum, silu_done, h_ready, d_psum, shared_added = sem("gu_psum"), sem("silu_done"), sem("h_ready"), sem("d_psum"), sem("shared_added")
        we_in = [sem(f"we_in{s}") for s in range(NBUF)]
        xs_in = [sem(f"xs_in{s}") for s in range(NBUF)]
        xsT_psum, xsT_out, egu_psum, esilu_done = sem("xsT_psum"), sem("xsT_out"), sem("egu_psum"), sem("esilu_done")
        eh_ready, ed_psum, ys_ready = sem("eh_ready"), sem("ed_psum"), sem("ys_ready")
        ys_out = [sem(f"ys_out{s}") for s in range(2)]
        xb_in = [sem(f"xb_in{s}") for s in range(2)]
        token_ready, base_stored, xb_init = sem("token_ready"), sem("base_stored"), sem("xb_init")
        parted = [sem(f"parted{i}") for i in range(2)]

        block = ctx.enter_context(nc.Block())

        def batches(eng, body):
            body(0, 0, 0)
            body(0, 1, 1)
            with eng.Fori(1, B // 2 - 1) as i:
                body(i, 0, None)
                body(i, 1, None)
            body(B // 2 - 1, 0, B - 2)
            body(B // 2 - 1, 1, B - 1)

        def unit_at(q, s, k):
            if k >= 0:
                return q, s, k
            return (q, 0, k + UB) if s else (q - 1, 1, k + UB)

        def slot_tiles(eng, body):
            for j in range(NBUF):
                body(0, j, j)
            with eng.Fori(1, NT // NBUF) as i:
                for r in range(NBUF):
                    body(i, r, None)
            for j in range(NBUF * (NT // NBUF), NT):
                body(j // NBUF, j % NBUF, j)

        @block.sync
        def _(sp):
            def load_batch(b):
                s = b % 2
                sp.dma_start(ctx_in[s][:, :, :], ctxT[b]).then_inc(in_ready[s], 16)
                sp.dma_start(x_in[s][:, :, :], x[b].rearrange("(t p) d -> p t d", p=P)).then_inc(in_ready[s], 16)
                sp.dma_start(mask_in[s][:, :, :], mask[b, 0].rearrange("(t p) k -> p t k", p=P)).then_inc(in_ready[s], 16)

            load_batch(0)
            sp.dma_start(w_qkvo[:, 0:3], wqkvoT[:, 0:3]).then_inc(w_attn_in, 16)
            sp.dma_start(b_qk[:, :, :], qkbias).then_inc(w_attn_in, 16)
            sp.dma_start(b_vo[:, :, :], vobias.rearrange("(o a) d -> o a d", o=1).to_broadcast([P, 2, D])).then_inc(w_attn_in, 16)
            load_batch(1)
            sp.dma_start(w_qkvo[:, 3:4], wqkvoT[:, 3:4]).then_inc(w_attn_rest_in, 16)
            sp.dma_start(w_r[:, :, :], wrT).then_inc(w_ffn_in, 16)
            sp.dma_start(w_gu[:, :, :], wguT).then_inc(w_ffn_in, 16)
            sp.dma_start(w_d[:, :, :], wdT).then_inc(w_ffn_in, 16)
            sp.wait_ge(zero_ready, 3)
            sp.dma_start(slots_in.rearrange("(j p) d -> p j d", p=P),
                         no_token[:, :].rearrange("p (o d) -> p o d", o=1).to_broadcast([P, NT, D + 1])).then_inc(slots_zeroed, 16)

            for b in range(B - 2):
                sp.wait_ge(kv_psum, b + 1)
                sp.wait_ge(xn_ready, 2 * (b + 1))
                sp.wait_ge(xres_ready, b + 1)
                sp.wait_ge(seen_ready, b + 1)
                load_batch(b + 2)

            sp.wait_ge(tile_e_ready, 1)

            w_size = P * wexp.shape[2]
            experts = wexp.rearrange("e p n -> (e p n)")

            def load_rows(j, s):
                sp.dma_start(xs[s][:, :], slots_in[bass.ds(j * P, P)]).then_inc(xs_in[s], 16)

            def load_weights(at, s):
                sp.dma_start(w_e[s][:, :], experts[bass.ds(at, w_size)].rearrange("(p n) -> p n", p=P)).then_inc(we_in[s], 16)

            def load_tile(j, s):
                at = sp.value_load(tile_w[0:1, bass.ds(j, 1)], min_val=0, max_val=(E - 1) * w_size)
                sp.wait_ge(ed_psum, j + (1 - NBUF))
                load_rows(j, s)
                load_weights(at, s)

            for j in range(NBUF):
                load_weights(sp.value_load(tile_w[0:1, j:j + 1], min_val=0, max_val=(E - 1) * w_size), j)

            def store_base(g):
                sp.wait_ge(shared_added, g + 1)
                sp.dma_start(base[g * S:(g + 1) * S].rearrange("(t p) d -> p t d", p=P),
                             x1[:, QT * g:QT * (g + 1), :]).then_inc(base_stored, 16)

            for g in range(B - 2):
                store_base(g)
            sp.wait_ge(scattered, 16 * NTT)
            for j in range(NBUF):
                load_rows(j, j)
            for g in range(B - 2, B):
                store_base(g)
            full = (NT - NBUF) // NBUF
            with sp.Fori(0, full) as i:
                for s in range(NBUF):
                    load_tile(NBUF * i + (NBUF + s), s)
            for s in range((NT - NBUF) % NBUF):
                load_tile(NBUF * (full + 1) + s, s)

        @block.gpsimd
        def _(pool):
            pool.memset(no_token[:, 0:D], 0.0).then_inc(zero_ready, 1)
            pool.iota(no_token[:, D:D + 1], pattern=[[0, 1]], base=T, channel_multiplier=1,
                      allow_small_or_imprecise_dtypes=True).then_inc(zero_ready, 1)
            pool.iota(xn2[:, :, D], pattern=[[P, NTT]], base=0, channel_multiplier=1,
                      allow_small_or_imprecise_dtypes=True).then_inc(zero_ready, 1)
            pool.memset(ident[:, :], 0.0).then_inc(const_base, 1)
            pool.memset(ones[:, :], 1.0).then_inc(const_base, 1)
            pool.memset(neghalf[:, :], -0.5).then_inc(const_ready, 1)
            pool.wait_ge(const_base, 2)
            pool.affine_select(out=ident[:, :], in_=ident[:, :], compare_op=ALU.not_equal, fill=1.0,
                               base=0, pattern=[[-1, P]], channel_multiplier=1).then_inc(const_ready, 1)
            pool.affine_select(out=before[:, :], in_=ones[:, :], compare_op=ALU.is_gt, fill=0.0,
                               base=0, pattern=[[1, P]], channel_multiplier=-1).then_inc(const_ready, 1)
            pool.affine_select(out=headblk[:, :], in_=ones[:, 0:HC], compare_op=ALU.is_ge, fill=0.0,
                               base=0, pattern=[[-HD, HC]], channel_multiplier=1).then_inc(const_base, 1)
            pool.wait_ge(const_base, 3)
            pool.affine_select(out=headblk[:, :], in_=headblk[:, :], compare_op=ALU.is_gt, fill=0.0,
                               base=HD, pattern=[[HD, HC]], channel_multiplier=-1).then_inc(const_ready, 1)
            pool.iota(rank_rev[:, :], pattern=[[-1, E]], base=E, channel_multiplier=0,
                      allow_small_or_imprecise_dtypes=True).then_inc(const_ready, 1)
            pool.iota(tile_lo[:, :], pattern=[[P, NTT]], base=0, channel_multiplier=0,
                      allow_small_or_imprecise_dtypes=True).then_inc(const_ready, 1)
            pool.iota(tile_no[:, :], pattern=[[1, NT]], base=0, channel_multiplier=0,
                      allow_small_or_imprecise_dtypes=True).then_inc(const_ready, 1)
            for s in range(2):
                pool.memset(vals[s][:, :, VP * HD:VW], 1.0).then_inc(const_ready, 1)
            pool.wait_ge(zero_ready, 3)
            pool.wait_ge(const_ready, 9)
            pool.tensor_copy(ident16[:, :], ident[:, :]).then_inc(const_ready, 1)
            pool.wait_ge(w_attn_in, 48)
            pool.wait_ge(const_ready, 10)
            pool.tensor_scalar(bq_scaled[:, :], b_qk[:, 0, :], SCALE, None, ALU.mult).then_inc(bq_ready, 1)

            def rstd_first(q, s):
                pool.wait_ge(ve_ready, 2 * q + (s + 1))
                pool.tensor_tensor(rstd[:, :], var_eps[:, :], neghalf[:, 0:QT], ALU.pow).then_inc(rstd_ready, 1)

            def rstd_second(q, s):
                pool.wait_ge(ve2_ready, 2 * q + (s + 1))
                pool.tensor_tensor(rstd2[:, :], var_eps2[:, :], neghalf[:, 0:QT], ALU.pow).then_inc(rstd2_ready, 1)

            def keep_residual(q, s):
                b = 2 * q + s
                pool.tensor_tensor(x1[:, bass.ds(QT * b, QT), :], x_in[s][:, :, :],
                                   b_vo[:, 1:2, :].to_broadcast([P, QT, D]), ALU.add).then_inc(xres_ready, 1)

            def spread_keys(q, s, c):
                b = 2 * q + s
                if c == 0:
                    pool.wait_ge(kv_out, DC * (b + 1))
                pool.tensor_tensor(kblk[s][:, c], kT[:, c:c + 1, :].to_broadcast([P, HC, K]),
                                   headblk[:, :].rearrange("p (h o) -> p h o", o=1).to_broadcast([P, HC, K]),
                                   ALU.mult).then_inc(kblk_ready, 1)

            def split_values(q, s, n, step):
                b = 2 * q + s
                part = lambda i: vals[s][:, :, i * HD:(i + 1) * HD]
                left = [val, *val_left]
                heads = lambda a: a[:, :].rearrange("k (h d) -> k h d", h=H)
                if step == 0:
                    pool.wait_ge(val_ready, b + 1)
                    if n not in (0, 1):
                        pool.wait_ge(pv_done, UB * (b - 1))
                    pool.tensor_tensor(part(0), heads(left[0]), heads(no_token[0:K, 0:D]), ALU.add).then_inc(val_step, 1)
                    pool.wait_ge(val_step, 3 * b + 1)
                    pool.tensor_tensor(heads(left[1]), heads(left[0]), part(0), ALU.subtract).then_inc(val_step, 1)
                else:
                    pool.wait_ge(val_step, 3 * b + 2)
                    pool.tensor_tensor(part(1), heads(left[1]), heads(no_token[0:K, 0:D]), ALU.add).then_inc(val_step, 1)
                    pool.wait_ge(val_step, 3 * b + 3)
                    pool.tensor_tensor(part(2), heads(left[1]), part(1), ALU.subtract).then_inc(vals_ready, 1)

            def shift(q, s, k):
                pool.wait_ge(s_top, UB * (2 * q + s) + (k + 1))
                pool.tensor_tensor(prob[k % 4][:, :, :], prob[k % 4][:, :, :],
                                   top[k % 4][:, :].rearrange("p (h o) -> p h o", o=1).to_broadcast([P, HU, K]),
                                   ALU.subtract).then_inc(s_shifted, 1)

            def low_part(q, s, k):
                pool.wait_ge(hi_ready, UB * (2 * q + s) + (k + 1))
                pool.tensor_tensor(prob_lo[k % 4][:, :, :], prob[k % 4][:, :, :], prob_hi[k % 4][:, :, :],
                                   ALU.subtract).then_inc(lo_ready, 1)

            def batch(q, s, n):
                nq, ns = (q + 1, 0) if s else (q, 1)
                for k in range(UB):
                    if k == 0 and n != B - 1:
                        rstd_first(nq, ns)
                    if k == 2 and n not in (0, 1):
                        rstd_second(q - 1, s)
                    shift(q, s, k)
                    if k >= 1 or n != 0:
                        low_part(*unit_at(q, s, k - 1))
                    if n == B - 1:
                        continue
                    if k in (2, 3):
                        spread_keys(nq, ns, k - 2)
                    if k == 4:
                        keep_residual(nq, ns)
                    if k in (5, 6):
                        split_values(nq, ns, None if n is None else n + 1, k - 5)

            rstd_first(0, 0)
            for c in range(DC):
                spread_keys(0, 0, c)
            keep_residual(0, 0)
            split_values(0, 0, 0, 0)
            split_values(0, 0, 0, 1)
            batches(pool, batch)
            low_part(B // 2 - 1, 1, UB - 1)
            rstd_second(B // 2 - 1, 0)
            rstd_second(B // 2 - 1, 1)

            pool.wait_ge(slot_ready, 1)
            pool.wait_ge(slots_zeroed, 16)
            pool.wait_ge(xs_ready, NTT)
            for t in range(NTT):
                pool.indirect_dma_start(slots_in, bass.IndirectOffsetOnAxis(ap=slot[:, t:t + 1], axis=0),
                                        xn2[:, t, :], None).then_inc(scattered, 16)

            tokens = out.rearrange("b s d -> (b s) d")

            def apart(i, j):
                if not isinstance(j, int) or j > 0:
                    pool.wait_ge(parted[i], j)
                pool.tensor_tensor(pool_carrier[:, i:i + 1], neghalf[0:1, 0:1], neghalf[0:1, 0:1], ALU.add).then_inc(parted[i], 1)

            def gather_base(j, s):
                pool.wait_ge(token_ready, j + 1)
                apart(0, j)
                pool.wait_ge(base_stored, 16 * B)
                pool.indirect_dma_start(xb[s % 2][:, :], None, base, bass.IndirectOffsetOnAxis(ap=token[s][:, 0:1], axis=0),
                                        bounds_check=T - 1, oob_is_err=False).then_inc(xb_in[s % 2], 16)

            def combine(q, s, j):
                if j is None or j < NT - 1:
                    gather_base(NBUF * q + (s + 1), (s + 1) % NBUF)
                pool.wait_ge(ys_ready, NBUF * q + (s + 1))
                apart(1, NBUF * q + s)
                pool.indirect_dma_start(tokens, bass.IndirectOffsetOnAxis(ap=token[s][:, 0:1], axis=0), ys[s % 2][:, :], None,
                                        bounds_check=T - 1, oob_is_err=False).then_inc(ys_out[s % 2], 16)

            for s in range(2):
                pool.memset(xb[s][:, :], 0.0).then_inc(xb_init, 1)
            pool.wait_ge(xb_init, 2)
            gather_base(0, 0)
            slot_tiles(pool, combine)
            pool.wait_ge(ys_out[0], 16 * ((NT + 1) // 2))
            pool.wait_ge(ys_out[1], 16 * (NT // 2))

        @block.tensor
        def _(pe):
            def project_kv(q, s):
                for c in range(DC):
                    for k in range(DC):
                        pe.matmul(ps[:, bank_m[0], c * K:(c + 1) * K], w_qkvo[:, 1, k, c * P:(c + 1) * P],
                                  ctx_in[s][:, k, :], start=(k == 0), stop=(k == DC - 1))
                for k in range(DC):
                    mm = pe.matmul(ps[0:K, bank_m[0], 2 * K:2 * K + D], ctx_in[s][:, k, :], w_qkvo[:, 2, k, :],
                                   start=(k == 0), stop=(k == DC - 1))
                mm.then_inc(kv_psum, 1)

            def transpose_xn(q, s):
                b = 2 * q + s
                pe.wait_ge(xn_ready, 2 * (b + 1))
                for c in range(DC):
                    for t in range(QT):
                        mm = pe.transpose(ps[:, bank_m[1], c * S + t * P:c * S + (t + 1) * P],
                                          xn[:, t, c * P:(c + 1) * P], ident[:, :])
                mm.then_inc(xnT_psum, 1)

            def project_q(q, s):
                b = 2 * q + s
                pe.wait_ge(val_ready, b + 1)
                pe.wait_ge(xnT_out, b + 1)
                for c in range(DC):
                    for k in range(DC):
                        mm = pe.matmul(ps[:, bank_m[0], c * S:(c + 1) * S], w_qkvo[:, 0, k, c * P:(c + 1) * P],
                                       xnT[:, k, :], start=(k == 0), stop=(k == DC - 1))
                mm.then_inc(q_psum, 1)

            def scores(q, s, k, started):
                b = 2 * q + s
                u = UB * b + k
                t, c, g = k // UT, (k // 2) % DC, k % 2
                if k == 0:
                    pe.wait_ge(q_out, DC * (b + 1))
                    pe.wait_ge(kblk_ready, DC * (b + 1))
                if started:
                    pe.wait_ge(s_masked, u - 1)
                pe.matmul(ps[:, bank_s[k % 2], 0:HU * K], qT[s][:, c, t * P:(t + 1) * P],
                          kblk[s][:, c, g * HU:(g + 1) * HU, :].rearrange("p h k -> p (h k)"),
                          start=True, stop=True).then_inc(s_psum, 1)

            def transpose_prob(q, s, k, started):
                u = UB * (2 * q + s) + k
                pe.wait_ge(lo_ready, u + 1)
                if started:
                    pe.wait_ge(pt_out, u - 1)
                bank = ps[0:K, bank_pt[k % 2], :].bitcast(F16)
                for i, part in enumerate((prob_hi, prob_lo)):
                    for h in range(HU):
                        mm = pe.transpose(bank[:, (i * HU + h) * P:(i * HU + h + 1) * P], part[k % 4][:, h, :], ident16[:, :])
                mm.then_inc(pt_psum, 1)

            def attend(q, s, k, started):
                b = 2 * q + s
                u = UB * b + k
                c, g = (k // 2) % DC, k % 2
                pe.wait_ge(pt_out, u + 1)
                if k == 0:
                    pe.wait_ge(vals_ready, b + 1)
                if g == 0 and started:
                    pe.wait_ge(att_ready, UB // 2 * b + (k // 2 - 1))
                for h in range(HU):
                    o = ps[:, bank_o[c], (g * HU + h) * VW:(g * HU + h + 1) * VW]
                    v = vals[s][:, c * HC + g * HU + h, :]
                    pe.matmul(o, probT[k % 2][:, 0, h, :], v, start=True, stop=False)
                    mm = pe.matmul(o, probT[k % 2][:, 1, h, :], v, start=False, stop=True)
                mm.then_inc(pv_done, 1)

            def transpose_att(q, s):
                b = 2 * q + s
                pe.wait_ge(att_ready, UB // 2 * (b + 1))
                for c in range(DC):
                    for t in range(QT):
                        mm = pe.transpose(ps[:, bank_m[1], c * S + t * P:c * S + (t + 1) * P],
                                          att[:, t, c * P:(c + 1) * P], ident[:, :])
                mm.then_inc(attT_psum, 1)

            def project_out(q, s):
                b = 2 * q + s
                pe.wait_ge(attT_out, b + 1)
                for t in range(QT):
                    for k in range(DC):
                        mm = pe.matmul(ps[:, bank_m[1], t * D:(t + 1) * D], attT[:, k, t * P:(t + 1) * P], w_qkvo[:, 3, k, :],
                                       start=(k == 0), stop=(k == DC - 1))
                mm.then_inc(y_psum, 1)

            def batch(q, s, n):
                b = 2 * q + s
                nq, ns = (q + 1, 0) if s else (q, 1)
                pq, pp = (q, 0) if s else (q - 1, 1)
                last = n == B - 1
                for k in range(UB):
                    if k < UB - 1:
                        scores(q, s, k + 1, n != 0 or k >= 1)
                    elif not last:
                        scores(nq, ns, 0, True)
                    if k >= T_LAG or n != 0:
                        transpose_prob(*unit_at(q, s, k - T_LAG), n != 0 or k >= T_LAG + 2)
                    if k >= V_LAG or n != 0:
                        attend(*unit_at(q, s, k - V_LAG), n != 0 or k >= V_LAG + 4)
                    if k == 0 and not last:
                        pe.wait_ge(in_ready[ns], 48 * (nq + 1))
                        pe.wait_ge(q_out, DC * (b + 1))
                        project_kv(nq, ns)
                    if k == 2 and not last:
                        if n not in (0, 1):
                            pe.wait_ge(x1_added, b - 1)
                        transpose_xn(nq, ns)
                    if k == 3 and not last:
                        project_q(nq, ns)
                    if k == 5 and n != 0:
                        if last:
                            pe.wait_ge(x1_added, b - 1)
                        else:
                            pe.wait_ge(xnT_out, b + 2)
                        transpose_att(pq, pp)
                    if k == 7 and n != 0:
                        project_out(pq, pp)

            pe.wait_ge(w_attn_in, 48)
            pe.wait_ge(in_ready[0], 48)
            project_kv(0, 0)
            pe.wait_ge(const_ready, 10)
            transpose_xn(0, 0)
            project_q(0, 0)
            scores(0, 0, 0, False)
            pe.wait_ge(w_attn_rest_in, 16)
            batches(pe, batch)
            q7 = B // 2 - 1
            for k in range(UB, UB + V_LAG):
                if k - T_LAG < UB:
                    transpose_prob(q7, 1, k - T_LAG, True)
                attend(q7, 1, k - V_LAG, True)
            pe.wait_ge(x1_added, B - 1)
            transpose_att(q7, 1)
            project_out(q7, 1)

            pe.wait_ge(w_ffn_in, 48)
            for g in range(B):
                pe.wait_ge(xn2_ready, QT * (g + 1))
                if g == 0:
                    pe.wait_ge(x1_added, B)
                    pe.wait_ge(att_ready, UB // 2 * B)
                if g >= 2:
                    pe.wait_ge(xn2T_out, g - 1)
                for c in range(DC):
                    for t in range(QT):
                        mm = pe.transpose(ps[:, bank_x[g % 2], c * S + t * P:c * S + (t + 1) * P],
                                          xn2[:, QT * g + t, c * P:(c + 1) * P], ident[:, :])
                mm.then_inc(xn2T_psum, 1)
                if g >= 1:
                    router_logits = g - 1
                    pe.wait_ge(xn2T_out, g)
                    for t in range(QT * router_logits, QT * g):
                        for k in range(DC):
                            pe.matmul(ps[:, bank_l, t * E:(t + 1) * E], xn2T[:, k, t * P:(t + 1) * P], w_r[:, k, :],
                                      start=(k == 0), stop=(k == DC - 1))
            pe.wait_ge(xn2T_out, B)
            for t in range(QT * (B - 1), NTT):
                for k in range(DC):
                    mm = pe.matmul(ps[:, bank_l, t * E:(t + 1) * E], xn2T[:, k, t * P:(t + 1) * P], w_r[:, k, :],
                                   start=(k == 0), stop=(k == DC - 1))
            mm.then_inc(l_psum, 1)

            def gate_up(g, n, first):
                if not first:
                    pe.wait_ge(h_ready, 2 * g - 1 + n)
                for part, bank in ((0, bank_g[n]), (1, bank_u[n])):
                    for m in range(2):
                        col = part * FF + (2 * n + m) * P
                        for k in range(DC):
                            mm = pe.matmul(ps[:, bank, m * S:(m + 1) * S], w_gu[:, k, col:col + P],
                                           xn2T[:, k, bass.ds(g * S, S)], start=(k == 0), stop=(k == DC - 1))
                    mm.then_inc(gu_psum, 1)

            def down(g, s, first):
                pe.wait_ge(h_ready, 2 * (g + 1))
                if not first:
                    pe.wait_ge(shared_added, g - 1)
                for t in range(QT):
                    for k in range(FC):
                        mm = pe.matmul(ps[:, bank_d[s], t * D:(t + 1) * D], hT[s][:, k, t * P:(t + 1) * P], w_d[:, k, :],
                                       start=(k == 0), stop=(k == FC - 1))
                mm.then_inc(d_psum, 1)

            gate_up(0, 0, True)
            gate_up(0, 1, True)
            pe.wait_ge(onehot_ready, 1)
            oh = onehot[:, :, :].rearrange("p t e -> p (t e)")
            pe.matmul(ps[:, bank_cnt, 0:NTT * E], before[:, :], oh, start=True, stop=True)
            pe.matmul(ps[:, bank_cnt, NTT * E:2 * NTT * E], ones[:, :], oh, start=True, stop=True).then_inc(cnt_psum, 1)

            def group(q, s, first, last):
                g = 2 * q + s
                if not first:
                    gate_up(g, 0, False)
                    if s == 1:
                        down(g - 1, 0, False)
                    else:
                        down(g - 1, 1, False)
                    gate_up(g, 1, False)

            gate_up(1, 0, False)
            pe.wait_ge(slot_ready, 1)
            down(0, 0, True)
            gate_up(1, 1, False)
            gate_up(2, 0, False)
            down(1, 1, True)
            gate_up(2, 1, False)
            with pe.Fori(0, (B - 4) // 2) as i:
                for r in range(2):
                    g = 2 * i + (3 + r)
                    gate_up(g, 0, False)
                    down(g - 1, r % 2, False)
                    gate_up(g, 1, False)
            gate_up(B - 1, 0, False)
            down(B - 2, 0, False)
            gate_up(B - 1, 1, False)
            down(B - 1, 1, False)

            def transpose_rows(j, s, xq, first2):
                pe.wait_ge(xs_in[s], 16 * (xq + 1))
                if not first2:
                    pe.wait_ge(xsT_out, j - 1)
                for c in range(DC):
                    mm = pe.transpose(ps[:, bank_x[s % 2], c * P:(c + 1) * P], xs[s][:, c * P:(c + 1) * P], ident[:, :])
                mm.then_inc(xsT_psum, 1)

            def expert_gate_up(j, s, q, first2):
                pe.wait_ge(we_in[s], 16 * (q + 1))
                pe.wait_ge(xsT_out, j + 1)
                if not first2:
                    pe.wait_ge(eh_ready, j - 1)
                for part, bank in ((0, bank_g[s % 2]), (1, bank_u[s % 2])):
                    for m in range(FC):
                        for k in range(DC):
                            col = k * 2 * FF + part * FF + m * P
                            mm = pe.matmul(ps[:, bank, m * P:(m + 1) * P], w_e[s][:, col:col + P], xsT[s % 2][:, k, :],
                                           start=(k == 0), stop=(k == DC - 1))
                    mm.then_inc(egu_psum, 1)

            def expert_down(j, s, first2):
                pe.wait_ge(eh_ready, j + 1)
                if not first2:
                    pe.wait_ge(ys_ready, j - 1)
                for k in range(FC):
                    col = DC * 2 * FF + k * D
                    mm = pe.matmul(ps[:, bank_d[s % 2], 0:D], hT[s % 2][:, k, 0:P], w_e[s][:, col:col + D],
                                   start=(k == 0), stop=(k == FC - 1))
                mm.then_inc(ed_psum, 1)

            pe.wait_ge(h_ready, 2 * B)
            pe.wait_ge(shared_added, B)

            def tile(q, s, j=None):
                j = NBUF * q + s if j is None else j
                transpose_rows(j, s, q, j in (0, 1) if isinstance(j, int) else False)
                if isinstance(j, int) and j == 0:
                    return
                expert_gate_up(j - 1, (s - 1) % NBUF, q - (s == 0), isinstance(j, int) and j <= 2)
                if isinstance(j, int) and j == 1:
                    return
                expert_down(j - 2, (s - 2) % NBUF, isinstance(j, int) and j <= 3)

            for j in range(NBUF):
                tile(0, j, j)
            rounds = NT // NBUF - 1
            with pe.Fori(1, 1 + rounds) as i:
                for r in range(NBUF):
                    tile(i, r)
            for j in range(NBUF * (1 + rounds), NT):
                tile(j // NBUF, j % NBUF, j)
            expert_gate_up(NT - 1, (NT - 1) % NBUF, (NT - 1) // NBUF, False)
            expert_down(NT - 2, (NT - 2) % NBUF, False)
            expert_down(NT - 1, (NT - 1) % NBUF, False)

        @block.scalar
        def _(act):
            def read_xnT(q, s):
                act.wait_ge(xnT_psum, 2 * q + (s + 1))
                act.activation(xnT[:, :, :].rearrange("p c n -> p (c n)"), ps[:, bank_m[1], :], ACT.Copy).then_inc(xnT_out, 1)

            def read_q(q, s):
                act.wait_ge(q_psum, 2 * q + (s + 1))
                for c in range(DC):
                    act.activation(qT[s][:, c, :], ps[:, bank_m[0], c * S:(c + 1) * S], ACT.Identity,
                                   bias=bq_scaled[:, c:c + 1], scale=SCALE).then_inc(q_out, 1)

            def read_attT(q, s):
                act.wait_ge(attT_psum, 2 * q + (s + 1))
                act.activation(attT[:, :, :].rearrange("p c n -> p (c n)"), ps[:, bank_m[1], :], ACT.Copy).then_inc(attT_out, 1)

            def exponential(q, s, k):
                act.wait_ge(s_shifted, UB * (2 * q + s) + (k + 1))
                act.activation(prob[k % 4][:, :, :], prob[k % 4][:, :, :], ACT.Exp).then_inc(exp_done, 1)

            def read_probT(q, s, k, started):
                u = UB * (2 * q + s) + k
                act.wait_ge(pt_psum, u + 1)
                if started:
                    act.wait_ge(pv_done, u - 1)
                act.activation(probT[k % 2][:, :, :, :].rearrange("p i h n -> p (i h n)"),
                               ps[0:K, bank_pt[k % 2], :].bitcast(F16), ACT.Copy).then_inc(pt_out, 1)

            def batch(q, s, n):
                nq, ns = (q + 1, 0) if s else (q, 1)
                pq, pp = (q, 0) if s else (q - 1, 1)
                for k in range(UB):
                    exponential(q, s, k)
                    if k >= T_LAG or n != 0:
                        read_probT(*unit_at(q, s, k - T_LAG), n != 0 or k >= T_LAG + 2)
                    if k == 2 and n != B - 1:
                        read_xnT(nq, ns)
                    if k == 3 and n != B - 1:
                        read_q(nq, ns)
                    if k == 5 and n != 0:
                        read_attT(pq, pp)

            act.wait_ge(bq_ready, 1)
            read_xnT(0, 0)
            read_q(0, 0)
            batches(act, batch)
            for k in range(UB, UB + T_LAG):
                read_probT(B // 2 - 1, 1, k - T_LAG, True)
            read_attT(B // 2 - 1, 1)

            for g in range(B):
                act.wait_ge(xn2T_psum, g + 1)
                act.activation(xn2T[:, :, g * S:(g + 1) * S], ps[:, bank_x[g % 2], :].rearrange("p (c n) -> p c n", c=DC),
                               ACT.Copy).then_inc(xn2T_out, 1)
            act.wait_ge(top_ready, 1)
            act.activation(eneg[:, :], top_l[:, :], ACT.Exp, scale=-1.0).then_inc(eneg_ready, 1)

            def silu(g, n, started):
                act.wait_ge(gu_psum, 4 * g + 2 * n + 1)
                if started:
                    act.wait_ge(h_ready, 2 * g - 1 + n)
                act.activation(act_g[n][:, :], ps[:, bank_g[n], :], ACT.Silu).then_inc(silu_done, 1)

            silu(0, 0, False)
            silu(0, 1, False)
            with act.Fori(1, B) as g:
                silu(g, 0, True)
                silu(g, 1, True)

            def tile(q, s, known):
                j = NBUF * q + s
                act.wait_ge(xsT_psum, j + 1)
                if known is None or known >= NBUF:
                    act.wait_ge(ys_out[s % 2], 32 * q + 16 * (s // 2 - 1))
                act.activation(token[s][:, :], xs[s][:, D:D + 1], ACT.Copy).then_inc(token_ready, 1)
                act.activation(xsT[s % 2][:, :, :].rearrange("p c n -> p (c n)"), ps[:, bank_x[s % 2], 0:DC * P],
                               ACT.Copy).then_inc(xsT_out, 1)
                if known != 0:
                    gate(j - 1, (s - 1) % 2)

            def gate(j, s):
                act.wait_ge(egu_psum, 2 * j + 1)
                act.activation(act_g[s][:, :], ps[:, bank_g[s], :], ACT.Silu).then_inc(esilu_done, 1)

            act.wait_ge(h_ready, 2 * B)
            slot_tiles(act, tile)
            gate(NT - 1, (NT - 1) % 2)

        @block.vector
        def _(dve):
            def apart():
                dve.memset(carrier[:, :], 0.0)

            def ln1_stats(q, s):
                b = 2 * q + s
                dve.wait_ge(in_ready[s], 48 * (q + 1))
                for t in range(QT):
                    dve.bn_stats(bn6[:, t, :], x_in[s][:, t, :]).then_inc(ln_step, 1)
                dve.wait_ge(ln_step, 4 * b + 2)
                apart()
                for t in range(QT):
                    dve.bn_aggr(mv[:, t, :], bn6[:, t, :]).then_inc(ln_step, 1)
                dve.wait_ge(ln_step, 4 * b + 4)
                dve.tensor_scalar(var_eps[:, :], mv[:, :, 1], EPS, None, ALU.add).then_inc(ve_ready, 1)

            def ln1_apply(q, s, started):
                b = 2 * q + s
                dve.wait_ge(rstd_ready, b + 1)
                if started:
                    dve.wait_ge(xnT_psum, b)
                for t in range(QT):
                    dve.tensor_scalar(xn[:, t, :], x_in[s][:, t, :], mv[:, t, 0:1], rstd[:, t:t + 1],
                                      ALU.subtract, ALU.mult).then_inc(xn_ready, 1)

            def read_mask(q, s):
                b = 2 * q + s
                dve.tensor_scalar(seen[:, :, :], mask_in[s][:, :, :], 0.0, VISIBLE, ALU.not_equal, ALU.mult).then_inc(seen_ready, 1)
                dve.wait_ge(seen_ready, b + 1)
                dve.tensor_scalar(cap[s][:, :, :], seen[:, :, :], MASKED, None, ALU.add).then_inc(cap_ready, 1)

            def read_kv(q, s, started):
                b = 2 * q + s
                dve.wait_ge(kv_psum, b + 1)
                if started:
                    dve.wait_ge(kblk_ready, DC * b)
                    dve.wait_ge(vals_ready, b)
                for c in range(DC):
                    dve.tensor_scalar(kT[:, c, :], ps[:, bank_m[0], c * K:(c + 1) * K], b_qk[:, 1, c:c + 1], None,
                                      ALU.add).then_inc(kv_out, 1)
                dve.tensor_tensor(val[:, :], ps[0:K, bank_m[0], 2 * K:2 * K + D], b_vo[0:K, 0, :], ALU.add).then_inc(val_ready, 1)

            def mask_scores(q, s, k, started):
                b = 2 * q + s
                u = UB * b + k
                t = k // UT
                if k == 0:
                    dve.wait_ge(cap_ready, b + 1)
                dve.wait_ge(s_psum, u + 1)
                if started:
                    dve.wait_ge(lo_ready, u - 3)
                dve.tensor_tensor(prob[k % 4][:, :, :], ps[:, bank_s[k % 2], 0:HU * K].rearrange("p (h k) -> p h k", h=HU),
                                  cap[s][:, t:t + 1, :].to_broadcast([P, HU, K]), ALU.min).then_inc(s_masked, 1)

            def find_top(q, s, k):
                dve.wait_ge(s_masked, UB * (2 * q + s) + (k + 1))
                dve.tensor_reduce(top[k % 4][:, :], prob[k % 4][:, :, :], AX_X, ALU.max).then_inc(s_top, 1)

            def high_part(q, s, k, started):
                u = UB * (2 * q + s) + k
                dve.wait_ge(exp_done, u + 1)
                if started:
                    dve.wait_ge(pt_psum, u - 3)
                dve.tensor_copy(prob_hi[k % 4][:, :, :], prob[k % 4][:, :, :]).then_inc(hi_ready, 1)

            def normalise(q, s, m, started=True):
                t, c = m // DC, m % DC
                n = QT * DC * (2 * q + s) + m
                o = ps[:, bank_o[c], 0:HC * VW].rearrange("p (h v) -> p h v", h=HC)
                dve.wait_ge(pv_done, 2 * n + 2)
                if m > 1 or started:
                    dve.wait_ge(att_ready, n - 1)
                dve.reciprocal(rden[m % 2][:, :], o[:, :, VP * HD]).then_inc(rden_ready, 1)
                dve.tensor_reduce(att_sum[m % 2][:, :, :], o[:, :, 0:VP * HD].rearrange("p h (i d) -> p h d i", i=VP),
                                  AX_X, ALU.add).then_inc(att_summed, 1)
                dve.wait_ge(rden_ready, n + 1)
                dve.wait_ge(att_summed, n + 1)
                if m == 0 and started:
                    dve.wait_ge(attT_psum, 2 * q + s)
                dve.tensor_tensor(att[:, t, c * P:(c + 1) * P].rearrange("p (h d) -> p h d", h=HC), att_sum[m % 2][:, :, :],
                                  rden[m % 2][:, :].rearrange("p (h o) -> p h o", o=1).to_broadcast([P, HC, HD]),
                                  ALU.mult).then_inc(att_ready, 1)

            def add_attention(q, s):
                b = 2 * q + s
                dve.wait_ge(y_psum, b + 1)
                dve.wait_ge(xres_ready, b + 1)
                here = x1[:, bass.ds(QT * b, QT), :]
                dve.tensor_tensor(here, ps[:, bank_m[1], :].rearrange("p (t d) -> p t d", t=QT), here, ALU.add).then_inc(x1_added, 1)
                dve.wait_ge(x1_added, b + 1)
                apart()
                for t in range(QT):
                    dve.bn_stats(bn6b[:, t, :], x1[:, bass.ds(QT * b + t, 1), :].rearrange("p o d -> p (o d)")).then_inc(ln2_step, 1)
                dve.wait_ge(ln2_step, 4 * b + 2)
                apart()
                for t in range(QT):
                    dve.bn_aggr(mvb[:, t, :], bn6b[:, t, :]).then_inc(ln2_step, 1)
                dve.wait_ge(ln2_step, 4 * b + 4)
                dve.tensor_scalar(var_eps2[:, :], mvb[:, :, 1], EPS, None, ALU.add).then_inc(ve2_ready, 1)

            def ln2_apply(q, s):
                b = 2 * q + s
                dve.wait_ge(rstd2_ready, b + 1)
                for t in range(QT):
                    dve.tensor_scalar(xn2[:, bass.ds(QT * b + t, 1), 0:D], x1[:, bass.ds(QT * b + t, 1), :], mvb[:, t, 0:1],
                                      rstd2[:, t:t + 1], ALU.subtract, ALU.mult).then_inc(xn2_ready, 1)

            def batch(q, s, n):
                nq, ns = (q + 1, 0) if s else (q, 1)
                pq, pp = (q, 0) if s else (q - 1, 1)
                last = n == B - 1
                for k in range(UB):
                    if k == 0 and not last:
                        ln1_stats(nq, ns)
                    mask_scores(q, s, k, n != 0 or k >= 4)
                    if k >= 1 or n != 0:
                        high_part(*unit_at(q, s, k - 1), n != 0 or k >= 5)
                    find_top(q, s, k)
                    if k == 0 and not last:
                        read_mask(nq, ns)
                    if k == 1 and not last:
                        ln1_apply(nq, ns, True)
                        read_kv(nq, ns, True)
                    if k == 1 and n not in (0, 1):
                        add_attention(q - 1, s)
                    if k == 3 and n not in (0, 1):
                        ln2_apply(q - 1, s)
                    if k in (0, 2, 4) and n != 0:
                        normalise(pq, pp, k // 2 + 1, n != 1 or k > 0)
                    if k == 6:
                        normalise(q, s, 0, n != 0)

            dve.wait_ge(w_attn_in, 48)
            dve.wait_ge(const_ready, 10)
            ln1_stats(0, 0)
            read_mask(0, 0)
            read_kv(0, 0, False)
            ln1_apply(0, 0, False)
            batches(dve, batch)
            q7 = B // 2 - 1
            high_part(q7, 1, UB - 1, True)
            normalise(q7, 1, 1)
            add_attention(q7, 0)
            normalise(q7, 1, 2)
            ln2_apply(q7, 0)
            normalise(q7, 1, 3)
            add_attention(q7, 1)
            ln2_apply(q7, 1)

            steps = [0]

            def step(ins):
                ins.then_inc(route_step, 1)
                steps[0] += 1
                dve.wait_ge(route_step, steps[0])

            def over_e(ap):
                return ap.rearrange("p (t o) -> p t o", o=1).to_broadcast([P, NTT, E])

            def over_t(ap):
                return ap.rearrange("p (o e) -> p o e", o=1).to_broadcast([P, NTT, E])

            dve.wait_ge(l_psum, 1)
            lp = ps[:, bank_l, 0:NTT * E].rearrange("p (t e) -> p t e", t=NTT)
            dve.tensor_reduce(top_l[:, :], lp, AX_X, ALU.max).then_inc(top_ready, 1)
            dve.wait_ge(top_ready, 1)
            step(dve.tensor_tensor(pick[:, :, :], lp, over_e(top_l[:, :]), ALU.is_equal))
            step(dve.tensor_tensor(logits[:, :, :], pick[:, :, :], over_t(rank_rev[:, :]), ALU.mult))
            step(dve.tensor_reduce(top_w[:, :], logits[:, :, :], AX_X, ALU.max))
            dve.tensor_tensor(onehot[:, :, :], over_t(rank_rev[:, :]), over_e(top_w[:, :]), ALU.is_equal).then_inc(onehot_ready, 1)
            dve.wait_ge(eneg_ready, 1)
            step(dve.tensor_scalar(eneg1[:, :], eneg[:, :], 1.0, None, ALU.add))
            step(dve.reciprocal(score[:, :], eneg1[:, :]))
            dve.wait_ge(xn2T_psum, B)
            for t in range(NTT):
                dve.tensor_scalar(xn2[:, t, 0:D], xn2[:, t, 0:D], score[:, t:t + 1], None, ALU.mult).then_inc(xs_ready, 1)

            def hidden_out(g, n, s):
                dve.wait_ge(silu_done, 2 * g + n + 1)
                dve.wait_ge(gu_psum, 4 * g + 2 * n + 2)
                dve.tensor_tensor(hT[s][:, 2 * n:2 * n + 2, :].rearrange("p m n -> p (m n)"), act_g[n][:, :],
                                  ps[:, bank_u[n], :], ALU.mult).then_inc(h_ready, 1)

            def add_shared(g, s):
                dve.wait_ge(d_psum, g + 1)
                here = x1[:, bass.ds(QT * g, QT), :]
                dve.tensor_tensor(here, ps[:, bank_d[s], :].rearrange("p (t d) -> p t d", t=QT), here, ALU.add).then_inc(shared_added, 1)

            hidden_out(0, 0, 0)
            hidden_out(0, 1, 0)

            dve.wait_ge(cnt_psum, 1)
            cnt = ps[:, bank_cnt, 0:NTT * E].rearrange("p (t e) -> p t e", t=NTT)
            all_ = ps[:, bank_cnt, NTT * E:2 * NTT * E].rearrange("p (t e) -> p e t", t=NTT)
            flat = lambda a: a[:, :, :].rearrange("p e t -> p (e t)")
            step(dve.tensor_copy(tot[:, :, :], all_))
            step(dve.tensor_tensor_scan(flat(upto), ones[:, 0:1].to_broadcast([P, E * NTT]), flat(tot), 0.0, ALU.mult, ALU.add))
            step(dve.tensor_tensor(prev[:, :, :], upto[:, :, :], tot[:, :, :], ALU.subtract))
            step(dve.tensor_reduce(n_e[:, :], tot[:, :, :], AX_X, ALU.add))
            step(dve.tensor_tensor(over[:, :, :], n_e[:, :].rearrange("p (e o) -> p e o", o=1).to_broadcast([P, E, NTT]),
                                   tile_lo[:, :].rearrange("p (o t) -> p o t", o=1).to_broadcast([P, E, NTT]), ALU.is_gt))
            step(dve.tensor_reduce(tiles_e[:, :], over[:, :, :], AX_X, ALU.add))
            step(dve.tensor_tensor_scan(upto_e[:, :], ones[:, 0:E], tiles_e[:, :], 0.0, ALU.mult, ALU.add))
            step(dve.tensor_tensor(le[:, :, :], upto_e[0:1, :].rearrange("p (o e) -> p o e", o=1).to_broadcast([1, NT, E]),
                                   tile_no[:, :].rearrange("p (j o) -> p j o", o=1).to_broadcast([1, NT, E]), ALU.is_le))
            step(dve.tensor_reduce(tile_e_f[:, :], le[:, :, :], AX_X, ALU.add))
            dve.tensor_scalar(tile_w[:, :], tile_e_f[:, :], float(E - 1), float(P * wexp.shape[2]), ALU.min, ALU.mult).then_inc(tile_e_ready, 1)
            step(dve.tensor_tensor(prev_e[:, :], upto_e[:, :], tiles_e[:, :], ALU.subtract))
            step(dve.scalar_tensor_tensor(adj[:, :], prev_e[:, :], float(P), prev[:, :, 0], ALU.mult, ALU.subtract))
            step(dve.tensor_tensor(off[:, :, :], cnt, prev[:, :, :].rearrange("p e t -> p t e"), ALU.add))
            step(dve.tensor_tensor(pick[:, :, :], off[:, :, :], over_t(adj[:, :]), ALU.add))
            step(dve.tensor_tensor(off[:, :, :], pick[:, :, :], onehot[:, :, :], ALU.mult))
            step(dve.tensor_reduce(slot_f[:, :], off[:, :, :], AX_X, ALU.add))
            dve.tensor_copy(slot[:, :], slot_f[:, :]).then_inc(slot_ready, 1)

            hidden_out(1, 0, 1)
            hidden_out(1, 1, 1)
            with dve.Fori(0, (B - 2) // 2) as i:
                for r in range(2):
                    g = 2 * i + (2 + r)
                    hidden_out(g, 0, r)
                    add_shared(g - 2, r)
                    hidden_out(g, 1, r)
            add_shared(B - 2, 0)
            add_shared(B - 1, 1)

            def expert_hidden(j, s, first2):
                dve.wait_ge(esilu_done, j + 1)
                dve.wait_ge(egu_psum, 2 * (j + 1))
                dve.tensor_tensor(hT[s % 2][:, :, 0:P], act_g[s % 2][:, :].rearrange("p (m n) -> p m n", m=FC),
                                  ps[:, bank_u[s % 2], :].rearrange("p (m n) -> p m n", m=FC), ALU.mult).then_inc(eh_ready, 1)

            def expert_rows(j, s, stored):
                dve.wait_ge(ed_psum, j + 1)
                if stored is not None:
                    dve.wait_ge(ys_out[s % 2], 16 * stored)
                    dve.wait_ge(xb_in[s % 2], 16 * (stored + 1))
                else:
                    dve.wait_ge(xb_in[s % 2], 16)
                dve.tensor_tensor(ys[s % 2][:, :], ps[:, bank_d[s % 2], 0:D], xb[s % 2][:, :], ALU.add).then_inc(ys_ready, 1)

            expert_hidden(0, 0, True)
            expert_hidden(1, 1, True)
            expert_rows(0, 0, None)
            expert_hidden(2, 0, False)
            expert_rows(1, 1, None)
            with dve.Fori(0, (NT - 3) // 2) as i:
                for r in range(2):
                    j = 2 * i + (3 + r)
                    expert_hidden(j, 1 - r, False)
                    expert_rows(j - 1, r, i + 1)
            expert_rows(NT - 1, 0, (NT - 1) // 2)


_OUT = ((8, 256, 256), "float32")


def _chunked(np, w, p=128):
    *lead, r, c = w.shape
    w = w.reshape(*lead, r // p, p, c)
    return np.ascontiguousarray(np.swapaxes(w, -3, -2))


def kernel(x, ctx_1024, mask_Bx1xSxS2_ik1, L0_xattn_Wq, L0_xattn_bq, L0_xattn_Wk, L0_xattn_bk, L0_xattn_Wv,
           L0_xattn_bv, L0_xattn_Wo, L0_xattn_bo, L0_ffn_w_router, L0_ffn_gate_up_proj, L0_ffn_down_proj,
           L0_ffn_w_gate, L0_ffn_w_up, L0_ffn_w_down):
    import numpy as np
    import concourse.bacc as bacc
    from concourse.bass_utils import run_bass_kernel_spmd

    a = np.asarray
    qkvo = np.stack([_chunked(np, a(w).T) for w in (L0_xattn_Wq, L0_xattn_Wk, L0_xattn_Wv, L0_xattn_Wo)], axis=1)
    gate_up = _chunked(np, a(L0_ffn_gate_up_proj))
    down = _chunked(np, a(L0_ffn_down_proj))
    experts = gate_up.shape[0]
    arrays = {
        "x": a(x),
        "ctxT": _chunked(np, np.swapaxes(a(ctx_1024), 1, 2)),
        "mask": a(mask_Bx1xSxS2_ik1),
        "w_qkvoT": qkvo,
        "qk_bias": np.stack([a(L0_xattn_bq).reshape(2, 128).T, a(L0_xattn_bk).reshape(2, 128).T], axis=1),
        "vo_bias": np.stack([a(L0_xattn_bv), a(L0_xattn_bo)]),
        "w_routerT": _chunked(np, a(L0_ffn_w_router).T),
        "w_gate_upT": _chunked(np, np.concatenate([a(L0_ffn_w_gate), a(L0_ffn_w_up)]).T),
        "w_downT": _chunked(np, a(L0_ffn_w_down).T),
        "w_experts": np.concatenate([gate_up.reshape(experts, 128, -1), down.reshape(experts, 128, -1)], axis=2),
    }
    nc = bacc.Bacc("TRN2", target_bir_lowering=False, num_devices=1)
    args = []
    for name, v in arrays.items():
        v = arrays[name] = np.ascontiguousarray(v)
        args.append(nc.dram_tensor(name, v.shape, mybir.dt.from_np(v.dtype), kind="ExternalInput").ap())
    args.append(nc.dram_tensor("out", _OUT[0], mybir.dt.from_np(np.dtype(_OUT[1])), kind="ExternalOutput").ap())
    xattn_moe(nc, *args)
    r = run_bass_kernel_spmd(nc, [arrays], core_ids=[0])
    return r.results[0]["out"]
```
